# Optimizing a Trainium2 kernel written in Bass

```python
import numpy as np
import jax
import jax.numpy as jnp

def _softmax(x, axis=-1):
    return jax.nn.softmax(x, axis=axis)

def _gelu(x):
    return jax.nn.gelu(x, approximate=True)

def _silu(x):
    return jax.nn.silu(x)

def _sigmoid(x):
    return jax.nn.sigmoid(x)

def _layernorm(x, axis=-1, eps=1e-05):
    m = jnp.mean(x, axis=axis, keepdims=True)
    v = jnp.var(x, axis=axis, keepdims=True)
    return (x - m) / jnp.sqrt(v + eps)

def _scatter_add(tgt, idx, src, axis=0):
    return tgt.at[idx].add(src)

def _segment_sum(src, seg, n):
    return jax.ops.segment_sum(src, seg, n)
kernel_name = 'mk_xattn_seq_d1_seqx_r4_cb2d96'

def setup_inputs(seed: int=0):
    np.random.seed(seed)
    _w = jnp.asarray

    def _rec_inputs():
        import jax
        import jax.numpy as jnp
        _rk = jax.random.key(seed)
        x = -0.0005207 + 1.001 * jax.random.normal(jax.random.fold_in(_rk, 1), (16, 512, 256), jnp.float32)
        _lenS = 512 - jax.random.randint(jax.random.fold_in(_rk, 7), (16,), 0, max(1, 512 // 4) + 1, jnp.int32)
        _lenS2 = 1601 - jax.random.randint(jax.random.fold_in(_rk, 8), (16,), 0, max(1, 1601 // 4) + 1, jnp.int32)
        _ctx_1024P = jax.random.normal(jax.random.fold_in(_rk, 11), (16, 16, 256), jnp.float32)
        _ctx_1024c = jax.random.dirichlet(jax.random.fold_in(_rk, 511), 0.3 * jnp.ones((16,), jnp.float32), (16, 1601))
        _ctx_1024t = jnp.einsum('bsk,bkd->bsd', _ctx_1024c, _ctx_1024P)
        _ctx_1024t = _ctx_1024t * jax.lax.rsqrt(jnp.mean(jnp.square(_ctx_1024t)) + 1e-12) * 0.953939
        ctx_1024 = 4.13588e-05 + 0.999923 * (_ctx_1024t + 0.3 * jax.random.normal(jax.random.fold_in(_rk, 611), (16, 1601, 256), jnp.float32))
        return (x, ctx_1024)
    x, ctx_1024 = _rec_inputs()

    def _L0_xattn_setup():
        import jax, jax.numpy as jnp
        import numpy as np
        D = 256
        H = 16
        DH = D // H
        FF = 4 * D
        EPS = 1e-05

        def _layer_norm(x, g, b):
            mu = jnp.mean(x, axis=-1, keepdims=True)
            var = jnp.mean(jnp.square(x - mu), axis=-1, keepdims=True)
            return (x - mu) * jax.lax.rsqrt(var + EPS) * g + b
        key = jax.random.key(seed)
        ks = jax.random.split(key, 12)
        B, Lq, Lkv = (2, 256, 1024)
        s = 1.0 / np.sqrt(D)
        sf = 1.0 / np.sqrt(FF)
        return {'Q': jax.random.normal(ks[0], (B, Lq, D), jnp.float32), 'KV': jax.random.normal(ks[1], (B, Lkv, D), jnp.float32), 'Wq': jax.random.normal(ks[2], (D, D), jnp.float32) * s, 'bq': jnp.zeros((D,), jnp.float32), 'Wk': jax.random.normal(ks[3], (D, D), jnp.float32) * s, 'bk': jnp.zeros((D,), jnp.float32), 'Wv': jax.random.normal(ks[4], (D, D), jnp.float32) * s, 'bv': jnp.zeros((D,), jnp.float32), 'Wo': jax.random.normal(ks[5], (D, D), jnp.float32) * s, 'bo': jnp.zeros((D,), jnp.float32), 'W1': jax.random.normal(ks[6], (D, FF), jnp.float32) * s, 'b1': jnp.zeros((FF,), jnp.float32), 'W2': jax.random.normal(ks[7], (FF, D), jnp.float32) * sf, 'b2': jnp.zeros((D,), jnp.float32), 'ln_q_g': jnp.ones((D,), jnp.float32), 'ln_q_b': jnp.zeros((D,), jnp.float32), 'ln_ff_g': jnp.ones((D,), jnp.float32), 'ln_ff_b': jnp.zeros((D,), jnp.float32)}
    _L0_xattn_all = _L0_xattn_setup()
    _L0_xattn_in = {k: v for k, v in _L0_xattn_all.items() if k in ('Wq', 'bq', 'Wk', 'bk', 'Wv', 'bv', 'Wo', 'bo', 'W1', 'b1', 'W2', 'b2', 'ln_q_g', 'ln_q_b', 'ln_ff_g', 'ln_ff_b')}
    del _L0_xattn_all
    return {'x': x, 'ctx_1024': ctx_1024, 'L0_xattn_Wq': _L0_xattn_in['Wq'], 'L0_xattn_bq': _L0_xattn_in['bq'], 'L0_xattn_Wk': _L0_xattn_in['Wk'], 'L0_xattn_bk': _L0_xattn_in['bk'], 'L0_xattn_Wv': _L0_xattn_in['Wv'], 'L0_xattn_bv': _L0_xattn_in['bv'], 'L0_xattn_Wo': _L0_xattn_in['Wo'], 'L0_xattn_bo': _L0_xattn_in['bo'], 'L0_xattn_W1': _L0_xattn_in['W1'], 'L0_xattn_b1': _L0_xattn_in['b1'], 'L0_xattn_W2': _L0_xattn_in['W2'], 'L0_xattn_b2': _L0_xattn_in['b2'], 'L0_xattn_ln_q_g': _L0_xattn_in['ln_q_g'], 'L0_xattn_ln_q_b': _L0_xattn_in['ln_q_b'], 'L0_xattn_ln_ff_g': _L0_xattn_in['ln_ff_g'], 'L0_xattn_ln_ff_b': _L0_xattn_in['ln_ff_b']}

def reference(x, ctx_1024, L0_xattn_Wq, L0_xattn_bq, L0_xattn_Wk, L0_xattn_bk, L0_xattn_Wv, L0_xattn_bv, L0_xattn_Wo, L0_xattn_bo, L0_xattn_W1, L0_xattn_b1, L0_xattn_W2, L0_xattn_b2, L0_xattn_ln_q_g, L0_xattn_ln_q_b, L0_xattn_ln_ff_g, L0_xattn_ln_ff_b):
    import jax
    import jax.numpy as jnp

    def _L0_xattn_ref(Q, KV, Wq, bq, Wk, bk, Wv, bv, Wo, bo, W1, b1, W2, b2, ln_q_g, ln_q_b, ln_ff_g, ln_ff_b):
        import jax, jax.numpy as jnp
        import numpy as np
        D = 256
        H = 16
        DH = D // H
        FF = 4 * D
        EPS = 1e-05

        def _layer_norm(x, g, b):
            mu = jnp.mean(x, axis=-1, keepdims=True)
            var = jnp.mean(jnp.square(x - mu), axis=-1, keepdims=True)
            return (x - mu) * jax.lax.rsqrt(var + EPS) * g + b
        B, Lq, _ = Q.shape
        Lkv = KV.shape[1]
        qn = _layer_norm(Q, ln_q_g, ln_q_b)
        q = (qn @ Wq + bq).reshape(B, Lq, H, DH).transpose(0, 2, 1, 3)
        k = (KV @ Wk + bk).reshape(B, Lkv, H, DH).transpose(0, 2, 1, 3)
        v = (KV @ Wv + bv).reshape(B, Lkv, H, DH).transpose(0, 2, 1, 3)
        scores = jnp.einsum('bhqd,bhkd->bhqk', q, k) / jnp.sqrt(jnp.float32(DH))
        attn = jax.nn.softmax(scores, axis=-1)
        ctx = jnp.einsum('bhqk,bhkd->bhqd', attn, v)
        ctx = ctx.transpose(0, 2, 1, 3).reshape(B, Lq, D)
        x = Q + (ctx @ Wo + bo)
        h = _layer_norm(x, ln_ff_g, ln_ff_b)
        ff = jax.nn.silu(h @ W1 + b1) @ W2 + b2
        return x + ff
    x = _L0_xattn_ref(x, ctx_1024, L0_xattn_Wq, L0_xattn_bq, L0_xattn_Wk, L0_xattn_bk, L0_xattn_Wv, L0_xattn_bv, L0_xattn_Wo, L0_xattn_bo, L0_xattn_W1, L0_xattn_b1, L0_xattn_W2, L0_xattn_b2, L0_xattn_ln_q_g, L0_xattn_ln_q_b, L0_xattn_ln_ff_g, L0_xattn_ln_ff_b)
    return x

_drawn_inputs = setup_inputs


def setup_inputs(seed=0):
    import zlib

    import numpy as np

    out = dict(_drawn_inputs(seed))
    spreads = {'L0_xattn_bq': (0.0, 0.403),
     'L0_xattn_bk': (0.0, 0.8),
     'L0_xattn_bv': (0.0, 0.1),
     'L0_xattn_bo': (0.0, 0.1),
     'L0_xattn_b1': (0.0, 0.1),
     'L0_xattn_b2': (0.0, 0.1),
     'L0_xattn_ln_q_g': (1.0, 0.2),
     'L0_xattn_ln_q_b': (0.0, 0.414),
     'L0_xattn_ln_ff_g': (1.0, 0.2),
     'L0_xattn_ln_ff_b': (0.0, 0.1)}
    factors = {}
    for name, (base, spread) in spreads.items():
        noise = np.random.default_rng([zlib.crc32(name.encode()), seed]).standard_normal(out[name].shape)
        drawn = base * np.exp(spread * noise) if base else spread * noise
        out[name] = jnp.asarray(drawn.astype(out[name].dtype))
    for name, factor in factors.items():
        out[name] = (out[name] * factor).astype(out[name].dtype)
    return out
```

```python
from contextlib import ExitStack

import concourse.bass as bass
from concourse import mybir

F32 = mybir.dt.float32
BF16 = mybir.dt.bfloat16
I32 = mybir.dt.int32
ACT = mybir.ActivationFunctionType
ALU = mybir.AluOpType
AX = mybir.AxisListType

P = 128
B, LQ, D = 16, 512, 256
LK = 1601
H, DH = 16, 16
FF = 1024
EPS = 1e-5
KC = D // P
FM = FF // P
KT = (LK + P - 1) // P
LAST = LK - (KT - 1) * P
CHUNK = 512
NCH = (LK + CHUNK - 1) // CHUNK
QT = LQ // P
HH = H // 2
GROUPS = 2
UNITS = GROUPS * KT * 2
PV_TILES = GROUPS * KT
PARTS = 3
K_ROWS = (0, 0, 0, 1, 1, 2)
Q_ROWS = (0, 1, 2, 0, 1, 0)
STACK = 16 * len(K_ROWS)
ROWS = STACK + PARTS
VH = DH + 1
VW = VH * (HH - 1) + 32
QH = LQ // 2
STACK_DMAS = 2 * HH * len(K_ROWS)


def keys_in(t):
    return P if t < KT - 1 else LAST


def width(c):
    return min(CHUNK, LK - c * CHUNK)


def tiles_in(c):
    return range(4 * c, min(4 * c + 4, KT))


TURN_CTX = [(u, "ctx", (c, kc)) for c, us in enumerate(((5, 6), (8, 9), (11, 12), (14, 15))) for kc, u in enumerate(us)]
PHASE1_STEPS = TURN_CTX + [(u, "k", c) for c, u in enumerate((16, 18, 20, 22))] \
    + [(u, "v", c) for c, u in enumerate((24, 26, 28, 30))] + [(31, "x", 0), (32, "x", 1), (34, "q", 0)]
PREP1 = [(u, "k", c) for c, u in enumerate((1, 3, 5, 7))] + [(9, "q", 0)] \
    + [(u, "v", c) for c, u in enumerate((11, 13, 15, 17))]
POST = [(4, "wo", 0), (8, "h", 0), (10, "w1", (0, 0)), (12, "w1", (0, 1)), (14, "w1", (0, 2)), (16, "w1", (0, 3)),
        (19, "w2", 0), (21, "wo", 1), (25, "h", 1), (28, "w1", (1, 0)), (31, "w1", (1, 1)), (34, "w1", (1, 2)),
        (37, "w1", (1, 3)), (41, "w2", 1)]
PHASE0_STEPS = sorted(PREP1 + POST, key=lambda s: s[0])
FIRST = len(PHASE1_STEPS) + len(PREP1)
PER_BATCH = len(PHASE1_STEPS) + len(PHASE0_STEPS)
assert FIRST % 2 == 0 and PER_BATCH % 2 == 0


def start1(b):
    return b, FIRST


def start0(b):
    return (b, len(PHASE1_STEPS)) if isinstance(b, int) and b == 0 else (b, FIRST - PER_BATCH + len(PHASE1_STEPS))


def bank(start, k):
    return (start[1] + k) % 2


def filled(start, k):
    return start[0] * PER_BATCH + (start[1] + k + 1)


def emptied(start, k):
    return start[0] * (PER_BATCH // 2) + ((start[1] + k) // 2 + 1)


def at(steps, u):
    return [(n, kind, arg) for n, (slot, kind, arg) in enumerate(steps) if slot == u]


def index(steps, kind, arg):
    return [(k, a) for _, k, a in steps].index((kind, arg))


class Tally:

    def __init__(self, sem):
        self.sem, self.start, self.here, self.loop = sem, 0, 0, None

    def inc(self, ins):
        self.here += 1
        ins.then_inc(self.sem, 1)

    @property
    def value(self):
        if self.loop is None:
            return self.start + self.here
        i, per = self.loop
        return i * per + (self.start + self.here)

    def enter(self, i, per):
        self.start, self.here, self.loop = self.start + self.here, 0, (i, per)

    def leave(self, rounds):
        assert self.here == self.loop[1], f"a round counts {self.here}"
        self.start, self.here, self.loop = self.start + self.here * rounds, 0, None


DVE_SEQ_PER_BATCH = 98
N_LOADS = 5 + 7 + 2 + 8


def xattn_kernel(nc, x, ctx, wq, bq, wk, bk, wv, bv, wo, bo, w1, b1, w2, b2, gq, cq, gf, cf, out):
    with ExitStack() as stack:
        def sb(name, shape, dt=F32):
            return stack.enter_context(nc.sbuf_tensor(name, shape, dt))

        def sem(name):
            return stack.enter_context(nc.semaphore(name))

        ident = sb("ident", [P, P])
        ones = sb("ones", [P, P])
        wq_sb = sb("wq_sb", [P, KC, D])
        wk_sb = sb("wk_sb", [P, KC, D])
        wv_sb = sb("wv_sb", [P, KC, D])
        wo_pad = sb("wo_pad", [P, 4, D])
        w1_sb = sb("w1_sb", [P, KC, FF])
        w2_sb = sb("w2_sb", [P, FM, D])
        bq_c = sb("bq_c", [P, KC])
        bk_c = sb("bk_c", [P, KC])
        bv_pad = sb("bv_pad", [P, 4])
        b1_c = sb("b1_c", [P, FM])
        half_b1 = sb("half_b1", [P, FM])
        gq_c, cq_c, gf_c, cf_c = (sb(n, [P, KC]) for n in ("gq_c", "cq_c", "gf_c", "cf_c"))
        bo_row = sb("bo_row", [P, D])
        b2_row = sb("b2_row", [P, D])
        ctx_nat = sb("ctx_nat", [P, 2, 4, D])
        ctxT = sb("ctxT", [P, KC, LK])
        x_nat = sb("x_nat", [P, QT, D])
        qnT = sb("qnT", [P, KC, LQ])
        whole = sb("whole", [P, 2, CHUNK])
        rest = sb("rest", [P, CHUNK])
        k_parts = sb("k_parts", [P, PARTS, LK], BF16)
        q_parts = sb("q_parts", [P, PARTS, LQ], BF16)
        k_stack = [sb(f"k_stack{s}", [ROWS, HH, LK], BF16) for s in range(2)]
        q_stack = [sb(f"q_stack{s}", [ROWS, HH, LQ], BF16) for s in range(2)]
        v_sb = [sb(f"v_sb{s}", [P, KT, VW]) for s in range(2)]
        neg_max = sb("neg_max", [P, QT, HH])
        shift_parts = q_parts[0:HH, :, :]
        probs = sb("probs", [P, 2, 4 * LQ])
        o_sb = sb("o_sb", [P, LQ])
        denom = sb("denom", [P, LQ])
        shift, shift_rest = o_sb[0:HH, :], denom[0:HH, :]
        attT = sb("attT", [P, 4, LQ])
        stats = sb("stats", [P, QT, 6])
        moments = sb("moments", [P, QT, 2])
        rstd, half_var, newton = (sb(n, [P, QT]) for n in ("rstd", "half_var", "newton"))
        xb = sb("xb", [P, 2, D])
        x1 = sb("x1", [P, 2, D])
        h_nat = sb("h_nat", [P, 2, D])
        hT = sb("hT", [P, KC, QH])
        tanh_sb = sb("tanh_sb", [P, 2, 2 * QH])
        ffT = sb("ffT", [P, FM, QH])
        y_sb = x_nat

        scores = stack.enter_context(nc.psum_tensor("scores", [P, 4 * LQ], F32))
        o_ps = stack.enter_context(nc.psum_tensor("o_ps", [P, 2, LQ], F32))
        side = stack.enter_context(nc.psum_tensor("side", [P, 2, CHUNK], F32))

        loaded = sem("loaded")
        zeroed = sem("zeroed")
        ident_made = sem("ident_made")
        bv_spread = sem("bv_spread")
        bo_made_ps = sem("bo_made_ps")
        bo_made = sem("bo_made")
        setup_done = sem("setup_done")
        ones_set = sem("ones_set")
        ctx_landed = [sem(f"ctx_landed{i}") for i in range(2)]
        x_landed = sem("x_landed")
        xn_ready = sem("xn_ready")
        side_ready = sem("side_ready")
        side_read = [sem(f"side_read{i}") for i in range(2)]
        split = sem("split")
        stack_landed = [sem(f"stack_landed{s}") for s in range(2)]
        scores_ready = sem("scores_ready")
        exp_done = sem("exp_done")
        pv_done = sem("pv_done")
        o_copied = sem("o_copied")
        att_ready = sem("att_ready")
        max_scores = sem("max_scores")
        max_found = sem("max_found")
        max_negated = sem("max_negated")
        max_turned = sem("max_turned")
        shift_split = sem("shift_split")
        shift_landed = sem("shift_landed")
        xb_landed = sem("xb_landed")
        xb_ready = sem("xb_ready")
        h_ready = sem("h_ready")
        x1_biased = sem("x1_biased")
        silu_done = sem("silu_done")
        y_stored = sem("y_stored")
        dve_seq = sem("dve_seq")

        passed = sem("passed")

        def wait_apart(eng, sem, value):
            eng.wait_ge(sem, value)
            if not isinstance(value, int):
                eng.sem_inc(passed, 1)

        block = stack.enter_context(nc.Block())

        @block.sync
        def _(sp):
            def column(dst, src, n):
                with nc.allow_non_contiguous_dma(reason="a bias, once"):
                    sp.dma_start(dst[:, 0:n], src.rearrange("(c p) -> p c", p=P)).then_inc(loaded, 16)

            def load_ctx(b, c):
                m = min(4, KT - 4 * c)
                if c < NCH - 1:
                    src = ctx[b, CHUNK * c:CHUNK * (c + 1), :].rearrange("(t p) d -> p t d", p=P)
                    sp.dma_start(ctx_nat[:, c % 2, :, :], src).then_inc(ctx_landed[c % 2], 16)
                else:
                    assert m == 1
                    sp.dma_start(ctx_nat[0:LAST, c % 2, 0, :], ctx[b, CHUNK * c:LK, :]).then_inc(ctx_landed[c % 2], 16)

            def load_x(b):
                sp.dma_start(x_nat[:, :, :], x[b].rearrange("(t p) d -> p t d", p=P)).then_inc(x_landed, 16)

            def load_xb(b, hf):
                sp.dma_start(xb[:, :, :], x[b, QH * hf:QH * (hf + 1), :].rearrange("(t p) d -> p t d", p=P))\
                    .then_inc(xb_landed, 16)

            def stack_k(b, s):
                if not (isinstance(b, int) and b == 0):
                    wait_apart(sp, scores_ready, (b * 2 + (s - 1)) * UNITS)
                sp.wait_ge(split, b * 10 + (5 * s + 4))
                for slot, part in enumerate(K_ROWS):
                    for h in range(HH):
                        sp.dma_start(k_stack[s][16 * slot:16 * slot + 16, h, :], k_parts[16 * h:16 * h + 16, part, :])\
                            .then_inc(stack_landed[s], 16)

            def stack_q(b, s):
                sp.wait_ge(split, b * 10 + (5 * s + 5))
                for slot, part in enumerate(Q_ROWS):
                    for h in range(HH):
                        sp.dma_start(q_stack[s][16 * slot:16 * slot + 16, h, :], q_parts[16 * h:16 * h + 16, part, :])\
                            .then_inc(stack_landed[s], 16)

            def place_shift(b, s):
                sp.wait_ge(shift_split, b * 2 + (s + 1))
                for i in range(PARTS):
                    sp.dma_start(q_stack[s][STACK + i:STACK + i + 1, :, :], shift_parts[:, i, :])\
                        .then_inc(shift_landed, 16)

            sp.dma_start(wk_sb[:, :, :], wk.rearrange("(c p) n -> p c n", p=P)).then_inc(loaded, 16)
            load_ctx(0, 0)
            load_ctx(0, 1)
            load_x(0)
            for dst, src in ((wq_sb, wq), (wv_sb, wv), (w1_sb, w1), (w2_sb, w2)):
                sp.dma_start(dst[:, :, :], src.rearrange("(c p) n -> p c n", p=P)).then_inc(loaded, 16)
            for dst, src, n in ((bq_c, bq, KC), (bk_c, bk, KC), (b1_c, b1, FM), (gq_c, gq, KC), (cq_c, cq, KC),
                                (gf_c, gf, KC), (cf_c, cf, KC)):
                column(dst, src, n)
            for dst, src in ((bo_row, bo), (b2_row, b2)):
                sp.dma_start(dst[:, :], src.partition_broadcast(P)).then_inc(loaded, 16)
            sp.wait_ge(zeroed, 2)
            for j in range(4):
                rows = wo.rearrange("(g j d) n -> j d g n", g=4, j=4)[j]
                sp.dma_start(wo_pad[32 * j:32 * j + 16, :, :], rows).then_inc(loaded, 16)
                with nc.allow_non_contiguous_dma(reason="a bias, once"):
                    sp.dma_start(bv_pad[32 * j:32 * j + 16, :], bv.rearrange("(g j d) -> j d g", g=4, j=4)[j])\
                        .then_inc(loaded, 16)
            for c in (2, 3):
                sp.wait_ge(side_ready, index(PHASE1_STEPS, "ctx", (c - 2, KC - 1)) + 1)
                load_ctx(0, c)
            stack_k(0, 0)
            stack_q(0, 0)

            def phase0(b, post):
                place_shift(b, 0)
                if post:
                    load_xb(b - 1, 0)
                stack_k(b, 1)
                stack_q(b, 1)
                if post:
                    finish(b - 1, start0(b), PHASE0_STEPS)

            def finish(b, start, steps):
                for hf in range(2):
                    if hf == 1:
                        wait_apart(sp, h_ready, b * 2 + 1)
                        load_xb(b, 1)
                    k = index(steps, "w2", hf)
                    wait_apart(sp, side_read[bank(start, k)], emptied(start, k))
                    sp.dma_start(out[b, QH * hf:QH * (hf + 1), :].rearrange("(t p) d -> p t d", p=P), y_sb[:, 2 * hf:2 * hf + 2, :])\
                        .then_inc(y_stored, 16)
                wait_apart(sp, y_stored, b * 32 + 32)

            def phase1(b, prepare):
                place_shift(b, 1)
                if prepare:
                    load_ctx(b + 1, 0)
                    load_ctx(b + 1, 1)
                    load_x(b + 1)
                    for c in (2, 3):
                        wait_apart(sp, side_ready, filled(start1(b), index(PHASE1_STEPS, "ctx", (c - 2, KC - 1))))
                        load_ctx(b + 1, c)
                    stack_k(b + 1, 0)
                    stack_q(b + 1, 0)

            phase0(0, False)
            with sp.Fori(0, B - 1) as i:
                phase1(i, True)
                phase0(i + 1, True)
            phase1(B - 1, False)
            load_xb(B - 1, 0)
            finish(B - 1, start1(B - 1), POST)
            sp.wait_ge(y_stored, 16 * 2 * B)

        @block.gpsimd
        def _(pool):
            pool.memset(wo_pad[:, :, :], 0.0).then_inc(zeroed, 1)
            pool.memset(bv_pad[:, :], 0.0).then_inc(zeroed, 1)
            pool.memset(ident[:, :], 0.0).then_inc(ident_made, 1)
            pool.wait_ge(ident_made, 1)
            pool.affine_select(out=ident[:, :], in_=ident[:, :], compare_op=ALU.not_equal, fill=1.0, base=0,
                               pattern=[[-1, P]], channel_multiplier=1).then_inc(ident_made, 1)
            for s in range(2):
                pool.memset(v_sb[s][:, :, :], 1.0).then_inc(ones_set, 1)
                pool.wait_ge(ones_set, 2 * s + 1)
                pool.memset(k_stack[s][STACK:ROWS, :, :], 1.0).then_inc(ones_set, 1)
                pool.wait_ge(ones_set, 2 * s + 2)

            pool.wait_ge(bo_made, 1)
            pool.wait_ge(loaded, 16 * N_LOADS)

            def finish(b):
                for hf in range(2):
                    pool.wait_ge(xb_landed, b * 32 + 16 * (hf + 1))
                    nc.gpsimd.tensor_tensor(xb[:, :, :], xb[:, :, :], bo_row[:, :].unsqueeze(1).broadcast_to((P, 2, D)),
                                            ALU.add).then_inc(xb_ready, 1)
                    pool.wait_ge(h_ready, b * 2 + (hf + 1))
                    nc.gpsimd.tensor_tensor(x1[:, :, :], x1[:, :, :], b2_row[:, :].unsqueeze(1).broadcast_to((P, 2, D)),
                                            ALU.add).then_inc(x1_biased, 1)

            with pool.Fori(0, B - 1) as i:
                finish(i)
            finish(B - 1)

        @block.scalar
        def _(act):
            act.wait_ge(loaded, 16 * N_LOADS)
            nc.scalar.mul(bq_c[:, :], bq_c[:, :], 1.0 / DH ** 0.5).then_inc(setup_done, 1)
            nc.scalar.mul(half_b1[:, :], b1_c[:, :], 0.5).then_inc(setup_done, 1)
            act.wait_ge(setup_done, 3)

            def split_input(b, s, start, k, use, w, bias, scale):
                act.wait_ge(side_ready, filled(start, k))
                if not (isinstance(b, int) and b * 10 + 5 * s + use < 2):
                    act.wait_ge(split, b * 10 + (5 * s + use - 1))
                nc.scalar.activation(whole[:, (5 * s + use) % 2, 0:w], side[:, bank(start, k), 0:w], ACT.Identity,
                                     bias=bias, scale=scale).then_inc(side_read[bank(start, k)], 1)

            def side_step(b, s, start, k, kind, arg):
                if kind == "k":
                    split_input(b, s, start, k, arg, width(arg), bk_c[:, s:s + 1], 1.0)
                elif kind == "q":
                    split_input(b, s, start, k, NCH, LQ, bq_c[:, s:s + 1], 1.0 / DH ** 0.5)
                elif kind == "w1":
                    hf, m2 = arg
                    bb = b - 1 if s == 1 else b
                    act.wait_ge(side_ready, filled(start, k))
                    act.wait_ge(silu_done, bb * 8 + (4 * hf + m2 + 1))
                    for half in range(2):
                        m = 2 * m2 + half
                        cols = slice(QH * half, QH * (half + 1))
                        nc.scalar.activation(ffT[:, m, :], side[:, bank(start, k), cols], ACT.Identity,
                                             bias=half_b1[:, m:m + 1], scale=0.5)
                        last = nc.scalar.activation(tanh_sb[:, m2 % 2, cols], side[:, bank(start, k), cols], ACT.Tanh,
                                                    bias=half_b1[:, m:m + 1], scale=0.5)
                    last.then_inc(side_read[bank(start, k)], 1)

            def phase(b, s, start, steps):
                for u in range(UNITS):
                    tile, pair = u // 2, u % 2
                    rows = keys_in(tile % KT)
                    act.wait_ge(scores_ready, b * (2 * UNITS) + (s * UNITS + u + 1))
                    if pair == 0 and not (isinstance(b, int) and b * 2 * PV_TILES + s * PV_TILES + tile < 2):
                        act.wait_ge(pv_done, b * (2 * PV_TILES) + (s * PV_TILES + tile - 1))
                    nc.scalar.activation(probs[0:rows, tile % 2, 2 * LQ * pair:2 * LQ * (pair + 1)],
                                         scores[0:rows, 2 * LQ * pair:2 * LQ * (pair + 1)], ACT.Exp)\
                        .then_inc(exp_done, 1)
                    for k, kind, arg in at(steps, u - 1):
                        side_step(b + s, 1 - s, start, k, kind, arg)

            for k, (_, kind, arg) in enumerate(PHASE1_STEPS):
                side_step(0, 0, (0, 0), k, kind, arg)
            phase(0, 0, start0(0), PREP1)
            with act.Fori(0, B - 1) as i:
                phase(i, 1, start1(i), PHASE1_STEPS)
                phase(i + 1, 0, start0(i + 1), PHASE0_STEPS)
            phase(B - 1, 1, start1(B - 1), [])
            for k, (_, kind, arg) in enumerate(POST):
                side_step(B, 1, start1(B - 1), k, kind, arg)

        @block.vector
        def _(dve):
            seq = Tally(dve_seq)

            def link(ins):
                seq.inc(ins)
                dve.wait_ge(dve_seq, seq.value)

            nc.vector.memset(ones[:, :], 1.0).then_inc(setup_done, 1)
            for n in range(2):
                nc.vector.memset(rstd[:, n:n + 1], 0.0).then_inc(silu_done, 1)
            dve.wait_ge(setup_done, 1)
            dve.wait_ge(loaded, 16 * N_LOADS)
            dve.wait_ge(setup_done, 3)
            dve.wait_ge(ones_set, 4)
            for g in range(4):
                nc.vector.tensor_scalar(probs[:, 0, P * g:P * (g + 1)], ones[:, :], bv_pad[:, g:g + 1], None,
                                        ALU.mult).then_inc(bv_spread, 1)
            dve.wait_ge(bo_made_ps, 1)
            nc.vector.tensor_tensor(bo_row[:, :], o_ps[:, 1, 0:D], bo_row[:, :], ALU.add).then_inc(bo_made, 1)

            def read_parts(b, s, k, start, use, parts, off, w):
                src = whole[:, (5 * s + use) % 2, 0:w]
                dve.wait_ge(side_read[bank(start, k)], emptied(start, k))
                link(nc.vector.tensor_copy(parts[:, 0, off:off + w], src))
                link(nc.vector.tensor_tensor(rest[:, 0:w], src, parts[:, 0, off:off + w], ALU.subtract))
                link(nc.vector.tensor_copy(parts[:, 1, off:off + w], rest[:, 0:w]))
                nc.vector.tensor_tensor(parts[:, 2, off:off + w], rest[:, 0:w], parts[:, 1, off:off + w],
                                        ALU.subtract).then_inc(split, 1)

            def inverse_root(variance, n):
                y, v, t = rstd[:, 0:n], half_var[:, 0:n], newton[:, 0:n]
                link(nc.vector.tensor_scalar(v, variance, EPS, None, ALU.add))
                link(nc.vector.tensor_scalar(y.bitcast(I32), v.bitcast(I32), -0.5, float(0x5F3759DF), ALU.mult, ALU.add))
                link(nc.vector.tensor_scalar(v, v, -0.5, None, ALU.mult))
                for _ in range(3):
                    link(nc.vector.tensor_tensor(t, y, y, ALU.mult))
                    link(nc.vector.tensor_tensor(t, t, v, ALU.mult))
                    link(nc.vector.scalar_tensor_tensor(y, t, 1.5, y, ALU.add, ALU.mult))

            def normalise(src, dst, tiles, ready):
                for t in range(tiles):
                    seq.inc(nc.vector.bn_stats(stats[:, t, :], src[:, t, :]))
                wait_apart(dve, dve_seq, seq.value)
                for t in range(tiles):
                    seq.inc(nc.vector.bn_aggr(moments[:, t, :], stats[:, t, :]))
                dve.wait_ge(dve_seq, seq.value)
                inverse_root(moments[:, 0:tiles, 1], tiles)
                for t in range(tiles):
                    last = nc.vector.tensor_scalar(dst[:, t, :], src[:, t, :], moments[:, t, 0:1], rstd[:, t:t + 1],
                                                   ALU.subtract, ALU.mult)
                last.then_inc(ready, 1)

            def side_step(b, s, start, k, kind, arg):
                bk_, first = bank(start, k), isinstance(b, int) and b == 0
                read, src = side_read[bk_], side[:, bk_, :]
                if kind in ("ctx", "x", "v", "h", "w2", "wo"):
                    dve.wait_ge(side_ready, filled(start, k))
                bb = b - 1 if s == 1 else b
                if kind == "ctx":
                    c, kc = arg
                    nc.vector.tensor_copy(ctxT[:, kc, CHUNK * c:CHUNK * c + width(c)], src[:, 0:width(c)])\
                        .then_inc(read, 1)
                elif kind == "x":
                    nc.vector.tensor_scalar(qnT[:, arg, :], src, gq_c[:, arg:arg + 1], cq_c[:, arg:arg + 1],
                                            ALU.mult, ALU.add).then_inc(read, 1)
                elif kind == "k":
                    if arg == 0 and not (first and s == 0):
                        dve.wait_ge(stack_landed[1 - s], b * (16 * STACK_DMAS) + 16 * STACK_DMAS * s)
                    read_parts(b, s, k, start, arg, k_parts, CHUNK * arg, width(arg))
                elif kind == "q":
                    read_parts(b, s, k, start, NCH, q_parts, 0, LQ)
                elif kind == "v":
                    if arg == 0 and not first:
                        dve.wait_ge(pv_done, b * (2 * PV_TILES) + (s - 1) * PV_TILES)
                    tiles, rows = tiles_in(arg), keys_in(tiles_in(arg)[-1])
                    dst = v_sb[s][0:rows, tiles[0]:tiles[-1] + 1, 0:VH * HH].rearrange("p t (h e) -> p t h e", e=VH)
                    nc.vector.tensor_copy(dst[:, :, :, 0:DH], side[0:rows, bk_, 0:P * len(tiles)].rearrange(
                        "p (t h e) -> p t h e", t=len(tiles), e=DH)).then_inc(read, 1)
                elif kind == "wo":
                    dve.wait_ge(xb_ready, bb * 2 + (arg + 1))
                    nc.vector.tensor_tensor(x1[:, :, :], src.rearrange("p (t d) -> p t d", d=D), xb[:, :, :],
                                            ALU.add).then_inc(read, 1)
                    dve.wait_ge(read, emptied(start, k))
                    normalise(x1, h_nat, 2, h_ready)
                elif kind == "h":
                    for kc in range(KC):
                        last = nc.vector.tensor_scalar(hT[:, kc, :], src[:, QH * kc:QH * (kc + 1)], gf_c[:, kc:kc + 1],
                                                       cf_c[:, kc:kc + 1], ALU.mult, ALU.add)
                    last.then_inc(read, 1)
                elif kind == "w1":
                    hf, m2 = arg
                    dve.wait_ge(read, emptied(start, k))
                    z = ffT[:, 2 * m2:2 * m2 + 2, :].rearrange("p m q -> p (m q)")
                    nc.vector.scalar_tensor_tensor(z, tanh_sb[:, m2 % 2, :], 1.0, z, ALU.add, ALU.mult)\
                        .then_inc(silu_done, 1)
                elif kind == "w2":
                    dve.wait_ge(x1_biased, bb * 2 + (arg + 1))
                    nc.vector.tensor_tensor(y_sb[:, 2 * arg:2 * arg + 2, :], src.rearrange("p (t d) -> p t d", d=D), x1[:, :, :],
                                            ALU.add).then_inc(read, 1)

            def normalise_x(b):
                dve.wait_ge(x_landed, b * 16 + 16)
                normalise(x_nat, x_nat, QT, xn_ready)

            def read_group(b, g):
                if not (isinstance(b, int) and b * 4 + g == 0):
                    dve.wait_ge(att_ready, b * 4 + g)
                dve.wait_ge(pv_done, b * (2 * PV_TILES) + KT * (g + 1))
                nc.vector.tensor_copy(o_sb[:, :], o_ps[:, g % 2, :]).then_inc(o_copied, 1)
                wait_apart(dve, o_copied, b * 4 + (g + 1))
                link(nc.vector.stream_shuffle(denom[:, :], o_sb[:, :], [DH] * 32))
                link(nc.vector.reciprocal(denom[:, :], denom[:, :]))
                nc.vector.tensor_tensor(attT[:, g, :], o_sb[:, :], denom[:, :], ALU.mult).then_inc(att_ready, 1)

            def row_maxima(b, s):
                for r in range(QT * HH):
                    t, h = r // HH, r % HH
                    dve.wait_ge(max_scores, b * (2 * QT * HH) + (s * QT * HH + r + 1))
                    nc.vector.tensor_reduce(neg_max[:, t, h:h + 1], scores[:, 0:LK], AX.X, ALU.max)\
                        .then_inc(max_found, 1)
                dve.wait_ge(max_found, b * (2 * QT * HH) + (s + 1) * QT * HH)
                nc.vector.tensor_scalar(neg_max[:, :, :], neg_max[:, :, :], -1.0, None, ALU.mult)\
                    .then_inc(max_negated, 1)
                dve.wait_ge(max_turned, b * 2 + (s + 1))
                link(nc.vector.tensor_copy(shift[:, :], scores[0:HH, 0:LQ]))
                link(nc.vector.tensor_copy(shift_parts[:, 0, :], shift[:, :]))
                link(nc.vector.tensor_tensor(shift_rest[:, :], shift[:, :], shift_parts[:, 0, :], ALU.subtract))
                link(nc.vector.tensor_copy(shift_parts[:, 1, :], shift_rest[:, :]))
                nc.vector.tensor_tensor(shift_parts[:, 2, :], shift_rest[:, :], shift_parts[:, 1, :],
                                        ALU.subtract).then_inc(shift_split, 1)

            def phase(b, s, start, steps):
                row_maxima(b, s)
                for u in range(UNITS):
                    if u == 2 and not (isinstance(b, int) and b == 0 and s == 0):
                        read_group(b - 1 + s, 3 - 2 * s)
                    if u == 2 + UNITS // 2:
                        read_group(b, 2 * s)
                    for k, kind, arg in at(steps, u):
                        if kind == "v" and arg == 0 and s == 1:
                            normalise_x(b + 1)
                        side_step(b + s, 1 - s, start, k, kind, arg)

            normalise_x(0)
            for k, (_, kind, arg) in enumerate(PHASE1_STEPS):
                side_step(0, 0, (0, 0), k, kind, arg)
            phase(0, 0, start0(0), PREP1)
            with dve.Fori(0, B - 1) as i:
                seq.enter(i, DVE_SEQ_PER_BATCH)
                phase(i, 1, start1(i), PHASE1_STEPS)
                phase(i + 1, 0, start0(i + 1), PHASE0_STEPS)
                seq.leave(B - 1)
            phase(B - 1, 1, start1(B - 1), [])
            read_group(B - 1, 3)
            for k, (_, kind, arg) in enumerate(POST):
                side_step(B, 1, start1(B - 1), k, kind, arg)

        @block.tensor
        def _(pe):
            pe.wait_ge(ident_made, 2)
            pe.wait_ge(loaded, 16 * N_LOADS)
            pe.wait_ge(bv_spread, 4)
            for g in range(4):
                last = nc.tensor.matmul(o_ps[:, 1, 0:D], probs[:, 0, P * g:P * (g + 1)], wo_pad[:, g, :],
                                        start=(g == 0), stop=(g == 3))
            last.then_inc(bo_made_ps, 1)
            pe.wait_ge(ones_set, 4)

            def side_step(b, s, start, k, kind, arg):
                number = start[1] + k
                if not (isinstance(start[0], int) and start[0] == 0 and number < 2):
                    pe.wait_ge(side_read[number % 2], emptied(start, k) - 1)
                bb = b - 1 if s == 1 else b
                dst = side[:, number % 2, :]

                def after(kind, arg, steps=PHASE1_STEPS):
                    j = index(steps, kind, arg)
                    pe.wait_ge(side_read[bank(start, j)], emptied(start, j))

                if kind == "ctx":
                    c, kc = arg
                    pe.wait_ge(ctx_landed[c % 2], b * 32 + 16 * (c // 2 + 1))
                    for t in tiles_in(c):
                        rows, j = keys_in(t), t - 4 * c
                        last = nc.tensor.transpose(dst[:, P * j:P * j + rows],
                                                   ctx_nat[0:rows, c % 2, j, P * kc:P * (kc + 1)],
                                                   ident[0:rows, 0:rows])
                elif kind == "x":
                    pe.wait_ge(xn_ready, b + 1)
                    for t in range(QT):
                        last = nc.tensor.transpose(dst[:, P * t:P * (t + 1)], x_nat[:, t, P * arg:P * (arg + 1)],
                                                   ident[:, :])
                elif kind == "k":
                    if s == 0:
                        for kc in range(KC):
                            after("ctx", (arg, kc))
                    for kc in range(KC):
                        last = nc.tensor.matmul(dst[:, 0:width(arg)], wk_sb[:, kc, P * s:P * (s + 1)],
                                                ctxT[:, kc, CHUNK * arg:CHUNK * arg + width(arg)],
                                                start=(kc == 0), stop=(kc == KC - 1))
                elif kind == "q":
                    if s == 0:
                        for kc in range(KC):
                            after("x", kc)
                    for kc in range(KC):
                        last = nc.tensor.matmul(dst, wq_sb[:, kc, P * s:P * (s + 1)], qnT[:, kc, :],
                                                start=(kc == 0), stop=(kc == KC - 1))
                elif kind == "v":
                    for t in tiles_in(arg):
                        rows, j = keys_in(t), t - 4 * arg
                        for kc in range(KC):
                            last = nc.tensor.matmul(dst[0:rows, P * j:P * (j + 1)], ctxT[:, kc, P * t:P * t + rows],
                                                    wv_sb[:, kc, P * s:P * (s + 1)], start=(kc == 0), stop=(kc == KC - 1))
                elif kind == "wo":
                    pe.wait_ge(att_ready, bb * 4 + 4)
                    for t in range(2):
                        for g in range(4):
                            q0 = QH * arg + P * t
                            last = nc.tensor.matmul(dst[:, D * t:D * (t + 1)], attT[:, g, q0:q0 + P], wo_pad[:, g, :],
                                                    start=(g == 0), stop=(g == 3))
                elif kind == "h":
                    pe.wait_ge(h_ready, bb * 2 + (arg + 1))
                    for kc in range(KC):
                        for t in range(2):
                            last = nc.tensor.transpose(dst[:, QH * kc + P * t:QH * kc + P * (t + 1)],
                                                       h_nat[:, t, P * kc:P * (kc + 1)], ident[:, :])
                elif kind == "w1":
                    hf, m2 = arg
                    if m2 == 0:
                        after("h", hf, POST if isinstance(b, int) and b == B else PHASE0_STEPS)
                    for half in range(2):
                        m = 2 * m2 + half
                        for kc in range(KC):
                            last = nc.tensor.matmul(dst[:, QH * half:QH * (half + 1)], w1_sb[:, kc, P * m:P * (m + 1)],
                                                    hT[:, kc, :], start=(kc == 0), stop=(kc == KC - 1))
                elif kind == "w2":
                    pe.wait_ge(silu_done, bb * 8 + (4 * (arg + 1) + 2))
                    for t in range(2):
                        for m in range(FM):
                            last = nc.tensor.matmul(dst[:, D * t:D * (t + 1)], ffT[:, m, P * t:P * (t + 1)],
                                                    w2_sb[:, m, :], start=(m == 0), stop=(m == FM - 1))
                last.then_inc(side_ready, 1)

            def find_maxima(b, s):
                pe.wait_ge(stack_landed[s], b * (16 * STACK_DMAS) + 16 * STACK_DMAS)
                if not (isinstance(b, int) and b == 0 and s == 0):
                    pe.wait_ge(exp_done, b * (2 * UNITS) + s * UNITS)
                for r in range(QT * HH):
                    t, h = r // HH, r % HH
                    if not (isinstance(b, int) and b == 0 and s == 0 and r == 0):
                        pe.wait_ge(max_found, b * (2 * QT * HH) + (s * QT * HH + r))
                    for c in range(NCH):
                        keys = slice(CHUNK * c, CHUNK * c + width(c))
                        last = nc.tensor.matmul(scores[:, keys], q_stack[s][0:STACK, h, P * t:P * (t + 1)],
                                                k_stack[s][0:STACK, h, keys], start=True, stop=True)
                    last.then_inc(max_scores, 1)
                pe.wait_ge(max_negated, b * 2 + (s + 1))
                for t in range(QT):
                    last = nc.tensor.transpose(scores[0:HH, P * t:P * (t + 1)], neg_max[:, t, :], ident[:, :])
                last.then_inc(max_turned, 1)
                pe.wait_ge(shift_landed, b * (32 * PARTS) + 16 * PARTS * (s + 1))

            def make_scores(b, s, u):
                tile, pair = u // 2, u % 2
                g, t = tile // KT, tile % KT
                if not (isinstance(b, int) and b == 0 and s == 0 and u < 2):
                    pe.wait_ge(exp_done, b * (2 * UNITS) + (s * UNITS + u - 1))
                for j in (2 * pair, 2 * pair + 1):
                    h = 4 * g + j
                    last = nc.tensor.matmul(scores[0:keys_in(t), LQ * j:LQ * (j + 1)],
                                            k_stack[s][:, h, P * t:P * t + keys_in(t)], q_stack[s][:, h, :],
                                            start=True, stop=True)
                last.then_inc(scores_ready, 1)

            def multiply_v(b, s, tile):
                g, t = tile // KT, tile % KT
                pe.wait_ge(exp_done, b * (2 * UNITS) + (s * UNITS + 2 * tile + 2))
                if t == 0 and not (isinstance(b, int) and b == 0 and s == 0):
                    pe.wait_ge(o_copied, b * 4 + (2 * s + g - 1))
                rows = keys_in(t)
                for j in range(4):
                    col = VH * (4 * g + j)
                    last = nc.tensor.matmul(o_ps[32 * j:32 * j + 32, g, :], v_sb[s][0:rows, t, col:col + 32],
                                            probs[0:rows, tile % 2, LQ * j:LQ * (j + 1)],
                                            start=(t == 0), stop=(t == KT - 1))
                last.then_inc(pv_done, 1)

            def phase(b, s, start, steps):
                if not (isinstance(b, int) and b == 0 and s == 0):
                    multiply_v(b - 1 + s, 1 - s, PV_TILES - 1)
                find_maxima(b, s)
                for u in range(UNITS):
                    make_scores(b, s, u)
                    if u % 2 == 1 and u > 1:
                        multiply_v(b, s, u // 2 - 1)
                    for k, kind, arg in at(steps, u):
                        side_step(b + s, 1 - s, start, k, kind, arg)

            for k, (_, kind, arg) in enumerate(PHASE1_STEPS):
                side_step(0, 0, (0, 0), k, kind, arg)
            phase(0, 0, start0(0), PREP1)
            with pe.Fori(0, B - 1) as i:
                phase(i, 1, start1(i), PHASE1_STEPS)
                phase(i + 1, 0, start0(i + 1), PHASE0_STEPS)
            phase(B - 1, 1, start1(B - 1), [])
            multiply_v(B - 1, 1, PV_TILES - 1)
            for k, (_, kind, arg) in enumerate(POST):
                side_step(B, 1, start1(B - 1), k, kind, arg)


_W = "L0_xattn_"
_INS = ["x", "ctx_1024", _W + "Wq", _W + "bq", _W + "Wk", _W + "bk", _W + "Wv", _W + "bv", _W + "Wo", _W + "bo",
        _W + "W1", _W + "b1", _W + "W2", _W + "b2", _W + "ln_q_g", _W + "ln_q_b", _W + "ln_ff_g", _W + "ln_ff_b"]


def kernel(**inputs):
    import numpy as np
    import concourse.bacc as bacc
    from concourse.bass_utils import run_bass_kernel_spmd

    nc = bacc.Bacc("TRN2", target_bir_lowering=False, num_devices=1)
    arrays, args = {}, []
    for name in _INS:
        a = np.ascontiguousarray(inputs[name])
        arrays[f"in_{name}"] = a
        args.append(nc.dram_tensor(f"in_{name}", a.shape, mybir.dt.from_np(a.dtype), kind="ExternalInput").ap())
    args.append(nc.dram_tensor("out", (B, LQ, D), F32, kind="ExternalOutput").ap())
    xattn_kernel(nc, *args)
    return run_bass_kernel_spmd(nc, [arrays], core_ids=[0]).results[0]["out"]
```

```python
from contextlib import ExitStack

import concourse.bass as bass
from concourse import mybir

F32 = mybir.dt.float32
BF16 = mybir.dt.bfloat16
I32 = mybir.dt.int32
ACT = mybir.ActivationFunctionType
ALU = mybir.AluOpType
AX = mybir.AxisListType

P = 128
B, LQ, D = 16, 512, 256
LK = 1601
H, DH = 16, 16
FF = 1024
EPS = 1e-5
KC = D // P
FM = FF // P
KT = (LK + P - 1) // P
LAST = LK - (KT - 1) * P
CHUNK = 512
NCH = (LK + CHUNK - 1) // CHUNK
QT = LQ // P
HH = H // 2
UNITS = KT * 2
PARTS = 3
K_ROWS = (0, 0, 0, 1, 1, 2)
Q_ROWS = (0, 1, 2, 0, 1, 0)
STACK = 16 * len(K_ROWS)
ROWS = STACK + PARTS
VH = DH + 1
VW = VH * (HH - 1) + 32
QH = LQ // 2
PLACED = 2 * HH * PARTS
REPEATED = 2 * (len(K_ROWS) - PARTS)
N_LOADS = 5 + 7 + 2 + 8


def keys_in(t):
    return P if t < KT - 1 else LAST


def width(c):
    return min(CHUNK, LK - c * CHUNK)


def tiles_in(c):
    return range(4 * c, min(4 * c + 4, KT))


PREPARE = (
    [(u, "v", c) for c, u in enumerate((2, 4, 8, 9))],
    [(u, "ctx", (n // KC, n % KC)) for n, u in enumerate((1, 2, 3, 4, 6, 7, 8, 9))]
    + [(u, "k", c) for c, u in enumerate((11, 13, 15, 17))] + [(19, "x", 0), (20, "x", 1), (22, "q", 0)],
    [(u, "v", c) for c, u in enumerate((3, 6, 9, 12))],
    [(u, "k", c) for c, u in enumerate((4, 8, 12, 15))] + [(18, "q", 0)],
)
PREPARED = ((0, 1), (1, 0), (1, 0), (1, 1))
FINISH = (
    [(6, "wo", 0), (11, "h", 0)] + [(u, "w1", (0, m)) for m, u in enumerate((13, 15, 17, 19))]
    + [(22, "w2", 0), (25, "wo", 1)],
    [],
    [(1, "h", 1)] + [(u, "w1", (1, m)) for m, u in enumerate((4, 7, 10, 13))] + [(17, "w2", 1)],
    [],
)
BOTH = tuple(sorted(p + f, key=lambda step: step[0]) for p, f in zip(PREPARE, FINISH))
NONE = ([], [], [], [])
PER_BATCH = sum(map(len, BOTH))
BEFORE = sum(len(PREPARE[q]) for q in (1, 2, 3))
LATER = BEFORE + sum(map(len, PREPARE)) - PER_BATCH
EPILOGUE = FINISH[0] + FINISH[2]


def starts(first, quarters):
    return [first + sum(map(len, quarters[:q])) for q in range(4)]


def at(steps, u):
    return [(n, kind, arg) for n, (slot, kind, arg) in enumerate(steps) if slot == u]


def index(steps, kind, arg):
    return [(k, a) for _, k, a in steps].index((kind, arg))


M_ROWS = QT * 4
TAIL = width(NCH - 1)
M_STEPS = [step for r in range(M_ROWS) for step in [(r, c) for c in range(NCH - 1)] + [(r, None)] * (r % 4 == 3)]
M_QUOTA = [3, 3] + [1] * 5 + [3] * 12 + [2, 2, 1]
assert sum(M_QUOTA) == len(M_STEPS) and len(M_STEPS) % 2 == 0
TURN_UNIT = 23


def maxima_at(u):
    done = sum(M_QUOTA[:u])
    return range(done, done + (M_QUOTA[u] if u < len(M_QUOTA) else 0))


def wait(eng, sem, value):
    if not (isinstance(value, int) and value <= 0):
        eng.wait_ge(sem, value)


class Tally:

    def __init__(self, sem):
        self.sem, self.start, self.here, self.loop = sem, 0, 0, None

    def inc(self, ins):
        self.here += 1
        ins.then_inc(self.sem, 1)

    @property
    def value(self):
        if self.loop is None:
            return self.start + self.here
        i, per = self.loop
        return i * per + (self.start - per + self.here)

    def enter(self, i, per):
        self.start, self.here, self.loop = self.start + self.here, 0, (i, per)

    def leave(self, rounds):
        assert self.here == self.loop[1], f"a round counts {self.here}"
        self.start, self.here, self.loop = self.start + self.here * rounds, 0, None


DVE_SEQ_PER_BATCH = 72
POOL_SEQ_PER_BATCH = 20


def xattn_kernel(nc, x, ctx, wq, bq, wk, bk, wv, bv, wo, bo, w1, b1, w2, b2, gq, cq, gf, cf, out):
    with ExitStack() as stack:
        def sb(name, shape, dt=F32):
            return stack.enter_context(nc.sbuf_tensor(name, shape, dt))

        def sem(name):
            return stack.enter_context(nc.semaphore(name))

        ident = sb("ident", [P, P])
        wq_sb = sb("wq_sb", [P, KC, D])
        wk_sb = sb("wk_sb", [P, KC, D])
        wv_sb = sb("wv_sb", [P, KC, D])
        wo_pad = sb("wo_pad", [P, 4, D])
        w1_sb = sb("w1_sb", [P, KC, FF])
        w2_sb = sb("w2_sb", [P, FM, D])
        bq_c = sb("bq_c", [P, KC])
        bk_c = sb("bk_c", [P, KC])
        bv_pad = sb("bv_pad", [P, 4])
        b1_c = sb("b1_c", [P, FM])
        half_b1 = sb("half_b1", [P, FM])
        gq_c, cq_c, gf_c, cf_c = (sb(n, [P, KC]) for n in ("gq_c", "cq_c", "gf_c", "cf_c"))
        bo_row = sb("bo_row", [P, D])
        b2_row = sb("b2_row", [P, D])
        ctx_nat = sb("ctx_nat", [P, 2, 4, D])
        ctxT = sb("ctxT", [P, KC, LK])
        x_nat = sb("x_nat", [P, QT, D])
        qnT = sb("qnT", [P, KC, LQ])
        whole = sb("whole", [P, 2, CHUNK])
        rest = sb("rest", [P, CHUNK])
        k_parts = sb("k_parts", [P, PARTS, LK], BF16)
        q_parts = sb("q_parts", [P, PARTS, LQ], BF16)
        k_stack = [sb(f"k_stack{s}", [ROWS, HH, LK], BF16) for s in range(2)]
        q_stack = [sb(f"q_stack{s}", [ROWS, HH, LQ], BF16) for s in range(2)]
        v_sb = [sb(f"v_sb{s}", [P, KT, VW]) for s in range(2)]
        chunk_max = sb("chunk_max", [P, M_ROWS, NCH])
        neg_max = sb("neg_max", [P, M_ROWS])
        shift_parts = sb("shift_parts", [4, PARTS, LQ], BF16)
        probs = sb("probs", [P, 2, 4 * LQ])
        o_sb = sb("o_sb", [P, LQ])
        denom = sb("denom", [P, LQ])
        shift_rest = o_sb[0:4, :]
        attT = sb("attT", [P, 4, LQ])
        stats = sb("stats", [P, QT, 6])
        moments = sb("moments", [P, QT, 2])
        rstd, half_var, newton = (sb(n, [P, QT]) for n in ("rstd", "half_var", "newton"))
        xb = sb("xb", [P, 2, D])
        x1 = sb("x1", [P, 2, D])
        h_nat = sb("h_nat", [P, 2, D])
        hT = sb("hT", [P, KC, QH])
        tanh_sb = sb("tanh_sb", [P, 2 * QH])
        ffT = sb("ffT", [P, FM, QH])

        scores = stack.enter_context(nc.psum_tensor("scores", [P, 4 * LQ], F32))
        o_ps = stack.enter_context(nc.psum_tensor("o_ps", [P, LQ], F32))
        side = stack.enter_context(nc.psum_tensor("side", [P, CHUNK], F32))
        rows_ps = stack.enter_context(nc.psum_tensor("rows_ps", [P, 2, CHUNK], F32))

        loaded = sem("loaded")
        zeroed = sem("zeroed")
        ident_made = sem("ident_made")
        bv_spread = sem("bv_spread")
        bo_product = sem("bo_product")
        bo_made = sem("bo_made")
        setup_done = sem("setup_done")
        ones_set = sem("ones_set")
        ctx_landed = [sem(f"ctx_landed{i}") for i in range(2)]
        x_landed = sem("x_landed")
        xn_ready = sem("xn_ready")
        side_ready = sem("side_ready")
        side_read = sem("side_read")
        split = sem("split")
        pool_seq = sem("pool_seq")
        placed = [sem(f"placed{s}") for s in range(2)]
        stack_landed = [sem(f"stack_landed{s}") for s in range(2)]
        scores_ready = sem("scores_ready")
        exp_done = sem("exp_done")
        pv_done = sem("pv_done")
        o_copied = sem("o_copied")
        inverted = sem("inverted")
        att_ready = sem("att_ready")
        rows_ready = sem("rows_ready")
        rows_read = sem("rows_read")
        max_negated = sem("max_negated")
        max_turned = sem("max_turned")
        shift_split = sem("shift_split")
        shift_landed = sem("shift_landed")
        xb_landed = sem("xb_landed")
        xb_ready = sem("xb_ready")
        h_ready = sem("h_ready")
        x1_biased = sem("x1_biased")
        silu_done = sem("silu_done")
        y_stored = sem("y_stored")
        dve_seq = sem("dve_seq")
        passed = sem("passed")

        def wait_apart(eng, sem, value):
            wait(eng, sem, value)
            if not isinstance(value, int):
                eng.sem_inc(passed, 1)

        def step_value(start, k):
            b, c = start
            return b * PER_BATCH + (c + k + 1)

        def per_quarter(n, b, q, more):
            return b * (4 * n) + (n * q + more)

        def walk(eng, prologue, quarter, epilogue, tallies=()):
            prologue()
            for q, c in enumerate(starts(BEFORE, PREPARE)):
                quarter(0, q, (0, c), PREPARE[q])
            with eng.Fori(1, B - 1) as b:
                for tally, per in tallies:
                    tally.enter(b, per)
                for q, c in enumerate(starts(LATER, BOTH)):
                    quarter(b, q, (b, c), BOTH[q])
                for tally, _ in tallies:
                    tally.leave(B - 2)
            last = (BOTH[0],) + NONE[:1] + (FINISH[2],) + NONE[:1]
            for q, c in enumerate(starts(LATER, last)):
                quarter(B - 1, q, (B - 1, c), last[q])
            epilogue((B - 1, LATER + sum(map(len, last))))

        block = stack.enter_context(nc.Block())

        @block.sync
        def _(sp):
            def column(dst, src, n):
                with nc.allow_non_contiguous_dma(reason="a bias, once"):
                    sp.dma_start(dst[:, 0:n], src.rearrange("(c p) -> p c", p=P)).then_inc(loaded, 16)

            def load_ctx(b, c):
                if c < NCH - 1:
                    src = ctx[b, CHUNK * c:CHUNK * (c + 1), :].rearrange("(t p) d -> p t d", p=P)
                    sp.dma_start(ctx_nat[:, c % 2, :, :], src).then_inc(ctx_landed[c % 2], 16)
                else:
                    sp.dma_start(ctx_nat[0:LAST, c % 2, 0, :], ctx[b, CHUNK * c:LK, :]).then_inc(ctx_landed[c % 2], 16)

            def load_x(b):
                sp.dma_start(x_nat[:, :, :], x[b].rearrange("(t p) d -> p t d", p=P)).then_inc(x_landed, 16)

            def load_xb(b, hf):
                sp.dma_start(xb[:, :, :], x[b, QH * hf:QH * (hf + 1), :].rearrange("(t p) d -> p t d", p=P))\
                    .then_inc(xb_landed, 16)

            def place(dst, src, rows, s):
                for part in range(PARTS):
                    slot = rows.index(part)
                    for h in range(HH):
                        sp.dma_start(dst[16 * slot:16 * slot + 16, h, :], src[16 * h:16 * h + 16, part, :])\
                            .then_inc(placed[s], 16)

            def repeat(dst, rows, s):
                for slot, part in enumerate(rows):
                    first = rows.index(part)
                    if slot != first:
                        sp.dma_start(dst[16 * slot:16 * slot + 16, :, :], dst[16 * first:16 * first + 16, :, :])\
                            .then_inc(stack_landed[s], 16)

            def fill_stacks(b, s):
                wait_apart(sp, scores_ready, per_quarter(UNITS, b, 2 * s - 2, 0))
                wait_apart(sp, split, b * 10 + (5 * s + 4))
                place(k_stack[s], k_parts, K_ROWS, s)
                wait_apart(sp, split, b * 10 + (5 * s + 5))
                place(q_stack[s], q_parts, Q_ROWS, s)
                wait_apart(sp, placed[s], (b + 1) * (16 * PLACED))
                repeat(k_stack[s], K_ROWS, s)
                repeat(q_stack[s], Q_ROWS, s)

            def place_shift(b, q):
                wait_apart(sp, shift_split, per_quarter(1, b, q, 1))
                g = q % 2
                for i in range(PARTS):
                    sp.dma_start(q_stack[q // 2][STACK + i:STACK + i + 1, 4 * g:4 * g + 4, :], shift_parts[:, i, :])\
                        .then_inc(shift_landed, 16)

            def store_y(b, hf, start, k):
                wait_apart(sp, side_read, step_value(start, k))
                sp.dma_start(out[b, QH * hf:QH * (hf + 1), :].rearrange("(t p) d -> p t d", p=P), x1[:, :, :])\
                    .then_inc(y_stored, 16)

            def prologue():
                sp.dma_start(wk_sb[:, :, :], wk.rearrange("(c p) n -> p c n", p=P)).then_inc(loaded, 16)
                load_ctx(0, 0)
                load_ctx(0, 1)
                load_x(0)
                for dst, src in ((wq_sb, wq), (wv_sb, wv), (w1_sb, w1), (w2_sb, w2)):
                    sp.dma_start(dst[:, :, :], src.rearrange("(c p) n -> p c n", p=P)).then_inc(loaded, 16)
                for dst, src, n in ((bq_c, bq, KC), (bk_c, bk, KC), (b1_c, b1, FM), (gq_c, gq, KC), (cq_c, cq, KC),
                                    (gf_c, gf, KC), (cf_c, cf, KC)):
                    column(dst, src, n)
                for dst, src in ((bo_row, bo), (b2_row, b2)):
                    sp.dma_start(dst[:, :], src.partition_broadcast(P)).then_inc(loaded, 16)
                sp.wait_ge(zeroed, 2)
                for j in range(4):
                    rows = wo.rearrange("(g j d) n -> j d g n", g=4, j=4)[j]
                    sp.dma_start(wo_pad[32 * j:32 * j + 16, :, :], rows).then_inc(loaded, 16)
                    with nc.allow_non_contiguous_dma(reason="a bias, once"):
                        sp.dma_start(bv_pad[32 * j:32 * j + 16, :], bv.rearrange("(g j d) -> j d g", g=4, j=4)[j])\
                            .then_inc(loaded, 16)
                for c in (2, 3):
                    sp.wait_ge(side_ready, index(PREPARE[1], "ctx", (c - 2, KC - 1)) + 1)
                    load_ctx(0, c)
                fill_stacks(0, 0)
                place_shift(0, 0)

            def quarter(b, q, start, steps):
                kinds = [(kind, arg) for _, kind, arg in steps]
                if q == 0:
                    if ("wo", 0) in kinds:
                        load_xb(b - 1, 0)
                    fill_stacks(b, 1)
                    if ("wo", 1) in kinds:
                        wait_apart(sp, h_ready, (b - 1) * 2 + 1)
                        load_xb(b - 1, 1)
                        store_y(b - 1, 0, start, kinds.index(("w2", 0)))
                if q == 1 and ("ctx", (0, 0)) in kinds:
                    load_ctx(b + 1, 0)
                    load_ctx(b + 1, 1)
                    load_x(b + 1)
                    for c in (2, 3):
                        wait_apart(sp, side_ready, step_value(start, kinds.index(("ctx", (c - 2, KC - 1)))))
                        load_ctx(b + 1, c)
                if q == 2:
                    if ("v", 0) in kinds:
                        fill_stacks(b + 1, 0)
                    if ("w2", 1) in kinds:
                        store_y(b - 1, 1, start, kinds.index(("w2", 1)))
                        wait_apart(sp, y_stored, (b - 1) * 32 + 32)
                if q < 3:
                    place_shift(b, q + 1)
                elif not (isinstance(b, int) and b == B - 1):
                    place_shift(b + 1, 0)

            def epilogue(start):
                load_xb(B - 1, 0)
                sp.wait_ge(h_ready, (B - 1) * 2 + 1)
                load_xb(B - 1, 1)
                store_y(B - 1, 0, start, index(EPILOGUE, "w2", 0))
                store_y(B - 1, 1, start, index(EPILOGUE, "w2", 1))
                sp.wait_ge(y_stored, 16 * 2 * B)

            walk(sp, prologue, quarter, epilogue)

        @block.gpsimd
        def _(pool):
            seq = Tally(pool_seq)

            def read_parts(b, s, start, k, use):
                n, w = 5 * s + use, width(use) if use < NCH else LQ
                parts, off = (k_parts, CHUNK * use) if use < NCH else (q_parts, 0)
                src, first, second = whole[:, n % 2, 0:w], parts[:, 0, off:off + w], parts[:, 1, off:off + w]
                pool.wait_ge(side_read, step_value(start, k))
                wait(pool, split, b * 10 + n)
                seq.inc(nc.gpsimd.tensor_tensor(rest[:, 0:w], src, first, ALU.subtract))
                seq.inc(nc.gpsimd.tensor_tensor(second, src, first, ALU.subtract))
                pool.wait_ge(pool_seq, seq.value)
                nc.gpsimd.tensor_tensor(parts[:, 2, off:off + w], rest[:, 0:w], second, ALU.subtract).then_inc(split, 1)

            def add_output_bias(b, hf):
                pool.wait_ge(xb_landed, b * 32 + 16 * (hf + 1))
                nc.gpsimd.tensor_tensor(xb[:, :, :], xb[:, :, :], bo_row[:, :].unsqueeze(1).broadcast_to((P, 2, D)),
                                        ALU.add).then_inc(xb_ready, 1)

            def add_mlp_bias(b, hf):
                pool.wait_ge(h_ready, b * 2 + (hf + 1))
                nc.gpsimd.tensor_tensor(x1[:, :, :], x1[:, :, :], b2_row[:, :].unsqueeze(1).broadcast_to((P, 2, D)),
                                        ALU.add).then_inc(x1_biased, 1)

            def scale_group(b, q):
                pool.wait_ge(inverted, per_quarter(1, b, q, 1))
                nc.gpsimd.tensor_tensor(attT[:, q, :], o_sb[:, :], denom[:, :], ALU.mult).then_inc(att_ready, 1)

            def splits(b, s, start, steps):
                for k, (_, kind, arg) in enumerate(steps):
                    if kind in ("k", "q"):
                        read_parts(b, s, start, k, arg if kind == "k" else NCH)

            def prologue():
                pool.memset(wo_pad[:, :, :], 0.0).then_inc(zeroed, 1)
                pool.memset(bv_pad[:, :], 0.0).then_inc(zeroed, 1)
                pool.memset(ident[:, :], 0.0).then_inc(ident_made, 1)
                pool.wait_ge(ident_made, 1)
                pool.affine_select(out=ident[:, :], in_=ident[:, :], compare_op=ALU.not_equal, fill=1.0, base=0,
                                   pattern=[[-1, P]], channel_multiplier=1).then_inc(ident_made, 1)
                for s in range(2):
                    pool.memset(v_sb[s][:, :, :], 1.0).then_inc(ones_set, 1)
                    pool.wait_ge(ones_set, 2 * s + 1)
                    pool.memset(k_stack[s][STACK:ROWS, :, :], 1.0).then_inc(ones_set, 1)
                    pool.wait_ge(ones_set, 2 * s + 2)
                pool.wait_ge(bo_made, 1)
                pool.wait_ge(loaded, 16 * N_LOADS)
                n = 0
                for q, (_, s) in ((1, PREPARED[1]), (2, PREPARED[2]), (3, PREPARED[3])):
                    splits(0, s, (0, n), PREPARE[q])
                    n += len(PREPARE[q])

            def quarter(b, q, start, steps):
                kinds = [(kind, arg) for _, kind, arg in steps]
                if q > 0:
                    scale_group(b, q - 1)
                elif not (isinstance(b, int) and b == 0):
                    scale_group(b - 1, 3)
                ahead, s = PREPARED[q]
                if ("wo", 0) in kinds:
                    add_output_bias(b - 1, 0)
                    add_mlp_bias(b - 1, 0)
                    add_output_bias(b - 1, 1)
                if ("w2", 1) in kinds:
                    add_mlp_bias(b - 1, 1)
                splits(b + ahead, s, start, steps)

            def epilogue(start):
                scale_group(B - 1, 3)
                for hf in range(2):
                    add_output_bias(B - 1, hf)
                    add_mlp_bias(B - 1, hf)

            walk(pool, prologue, quarter, epilogue, [(seq, POOL_SEQ_PER_BATCH)])

        @block.scalar
        def _(act):
            def side_step(b, s, start, k, kind, arg):
                if kind in ("wo", "w2"):
                    return
                act.wait_ge(side_ready, step_value(start, k))
                if kind == "ctx":
                    c, kc = arg
                    last = nc.scalar.copy(ctxT[:, kc, CHUNK * c:CHUNK * c + width(c)], side[:, 0:width(c)])
                elif kind == "x":
                    last = nc.scalar.activation(qnT[:, arg, :], side[:, :], ACT.Identity, bias=cq_c[:, arg:arg + 1],
                                                scale=gq_c[:, arg:arg + 1])
                elif kind == "h":
                    for kc in range(KC):
                        last = nc.scalar.activation(hT[:, kc, :], side[:, QH * kc:QH * (kc + 1)], ACT.Identity,
                                                    bias=cf_c[:, kc:kc + 1], scale=gf_c[:, kc:kc + 1])
                elif kind == "v":
                    if arg == 0:
                        wait(act, pv_done, per_quarter(KT, b, 2 * s - 2, 0))
                    tiles, rows = tiles_in(arg), keys_in(tiles_in(arg)[-1])
                    dst = v_sb[s][0:rows, tiles[0]:tiles[-1] + 1, 0:VH * HH].rearrange("p t (h e) -> p t h e", e=VH)
                    last = nc.scalar.copy(dst[:, :, :, 0:DH], side[0:rows, 0:P * len(tiles)].rearrange(
                        "p (t h e) -> p t h e", t=len(tiles), e=DH))
                elif kind in ("k", "q"):
                    use = arg if kind == "k" else NCH
                    n, w = 5 * s + use, width(use) if use < NCH else LQ
                    parts, off = (k_parts, CHUNK * use) if kind == "k" else (q_parts, 0)
                    bias, scale = (bk_c[:, s:s + 1], 1.0) if kind == "k" else (bq_c[:, s:s + 1], 1.0 / DH ** 0.5)
                    if kind == "k" and arg == 0:
                        wait(act, placed[1 - s], (b + s) * (16 * PLACED))
                    wait(act, split, b * 10 + (n - 1))
                    nc.scalar.activation(whole[:, n % 2, 0:w], side[:, 0:w], ACT.Identity, bias=bias, scale=scale)
                    last = nc.scalar.activation(parts[:, 0, off:off + w], side[:, 0:w], ACT.Identity, bias=bias,
                                                scale=scale)
                else:
                    hf, m2 = arg
                    if m2 > 0:
                        act.wait_ge(silu_done, b * 8 + (4 * hf + m2))
                    for half in range(2):
                        m = 2 * m2 + half
                        cols = slice(QH * half, QH * (half + 1))
                        nc.scalar.activation(ffT[:, m, :], side[:, cols], ACT.Identity, bias=half_b1[:, m:m + 1],
                                             scale=0.5)
                        last = nc.scalar.activation(tanh_sb[:, cols], side[:, cols], ACT.Tanh,
                                                    bias=half_b1[:, m:m + 1], scale=0.5)
                last.then_inc(side_read, 1)

            def copy_group(b, q):
                act.wait_ge(pv_done, per_quarter(KT, b, q, KT))
                wait(act, att_ready, per_quarter(1, b, q, 0))
                nc.scalar.copy(o_sb[:, :], o_ps[:, :]).then_inc(o_copied, 1)

            def prologue():
                act.wait_ge(loaded, 16 * N_LOADS)
                nc.scalar.mul(bq_c[:, :], bq_c[:, :], 1.0 / DH ** 0.5).then_inc(setup_done, 1)
                nc.scalar.mul(half_b1[:, :], b1_c[:, :], 0.5).then_inc(setup_done, 1)
                act.wait_ge(setup_done, 2)
                act.wait_ge(ones_set, 4)
                n = 0
                for q in (1, 2, 3):
                    for k, (_, kind, arg) in enumerate(PREPARE[q]):
                        side_step(0, PREPARED[q][1], (0, n), k, kind, arg)
                    n += len(PREPARE[q])

            def quarter(b, q, start, steps):
                ahead, s = PREPARED[q]
                for u in range(UNITS):
                    t, pair = u // 2, u % 2
                    rows = keys_in(t)
                    if u == 2:
                        if q > 0:
                            copy_group(b, q - 1)
                        elif not (isinstance(b, int) and b == 0):
                            copy_group(b - 1, 3)
                    act.wait_ge(scores_ready, per_quarter(UNITS, b, q, u + 1))
                    if pair == 0:
                        wait(act, pv_done, per_quarter(KT, b, q, t - 1))
                    nc.scalar.activation(probs[0:rows, (q + t) % 2, 2 * LQ * pair:2 * LQ * (pair + 1)],
                                         scores[0:rows, 2 * LQ * pair:2 * LQ * (pair + 1)], ACT.Exp)\
                        .then_inc(exp_done, 1)
                    for k, kind, arg in at(steps, u):
                        if kind in ("h", "w1"):
                            side_step(b - 1, None, start, k, kind, arg)
                        else:
                            side_step(b + ahead, s, start, k, kind, arg)

            def epilogue(start):
                copy_group(B - 1, 3)
                for k, (_, kind, arg) in enumerate(EPILOGUE):
                    side_step(B - 1, None, start, k, kind, arg)

            walk(act, prologue, quarter, epilogue)

        @block.vector
        def _(dve):
            seq = Tally(dve_seq)

            def link(ins):
                seq.inc(ins)
                dve.wait_ge(dve_seq, seq.value)

            def inverse_root(variance, n):
                y, v, t = rstd[:, 0:n], half_var[:, 0:n], newton[:, 0:n]
                link(nc.vector.tensor_scalar(v, variance, EPS, None, ALU.add))
                link(nc.vector.tensor_scalar(y.bitcast(I32), v.bitcast(I32), -0.5, float(0x5F3759DF), ALU.mult, ALU.add))
                link(nc.vector.tensor_scalar(v, v, -0.5, None, ALU.mult))
                for _ in range(3):
                    link(nc.vector.tensor_tensor(t, y, y, ALU.mult))
                    link(nc.vector.tensor_tensor(t, t, v, ALU.mult))
                    link(nc.vector.scalar_tensor_tensor(y, t, 1.5, y, ALU.add, ALU.mult))

            def normalise(src, dst, tiles, ready):
                for t in range(tiles):
                    seq.inc(nc.vector.bn_stats(stats[:, t, :], src[:, t, :]))
                wait_apart(dve, dve_seq, seq.value)
                for t in range(tiles):
                    seq.inc(nc.vector.bn_aggr(moments[:, t, :], stats[:, t, :]))
                dve.wait_ge(dve_seq, seq.value)
                inverse_root(moments[:, 0:tiles, 1], tiles)
                for t in range(tiles):
                    last = nc.vector.tensor_scalar(dst[:, t, :], src[:, t, :], moments[:, t, 0:1], rstd[:, t:t + 1],
                                                   ALU.subtract, ALU.mult)
                last.then_inc(ready, 1)

            def side_step(b, start, k, kind, arg):
                if kind in ("wo", "w2"):
                    dve.wait_ge(side_ready, step_value(start, k))
                if kind == "wo":
                    dve.wait_ge(xb_ready, b * 2 + (arg + 1))
                    if arg == 1:
                        dve.wait_ge(y_stored, b * 32 + 16)
                    nc.vector.tensor_tensor(x1[:, :, :], side[:, :].rearrange("p (t d) -> p t d", d=D), xb[:, :, :],
                                            ALU.add).then_inc(side_read, 1)
                    dve.wait_ge(side_read, step_value(start, k))
                    normalise(x1, h_nat, 2, h_ready)
                elif kind == "w1":
                    hf, m2 = arg
                    dve.wait_ge(side_read, step_value(start, k))
                    z = ffT[:, 2 * m2:2 * m2 + 2, :].rearrange("p m q -> p (m q)")
                    nc.vector.scalar_tensor_tensor(z, tanh_sb[:, :], 1.0, z, ALU.add, ALU.mult).then_inc(silu_done, 1)
                elif kind == "w2":
                    dve.wait_ge(x1_biased, b * 2 + (arg + 1))
                    nc.vector.tensor_tensor(x1[:, :, :], side[:, :].rearrange("p (t d) -> p t d", d=D), x1[:, :, :],
                                            ALU.add).then_inc(side_read, 1)

            def normalise_x(b):
                dve.wait_ge(x_landed, b * 16 + 16)
                normalise(x_nat, x_nat, QT, xn_ready)

            def spread_denominators(b, q):
                wait_apart(dve, o_copied, per_quarter(1, b, q, 1))
                link(nc.vector.stream_shuffle(denom[:, :], o_sb[:, :], [DH] * 32))

            def invert_denominators(piece):
                cols = slice(P * piece, P * (piece + 1))
                ins = nc.vector.reciprocal(denom[:, cols], denom[:, cols])
                if piece == QT - 1:
                    ins.then_inc(inverted, 1)

            def read_rows(b, q, m):
                r, c = M_STEPS[m]
                dve.wait_ge(rows_ready, per_quarter(len(M_STEPS), b, q, m + 1))
                if c is None:
                    dst = chunk_max[:, r - 3:r + 1, NCH - 1]
                    src = rows_ps[:, m % 2, 0:4 * TAIL].rearrange("p (r k) -> p r k", k=TAIL)
                else:
                    dst, src = chunk_max[:, r, c:c + 1], rows_ps[:, m % 2, :]
                nc.vector.tensor_reduce(dst, src, AX.X, ALU.max).then_inc(rows_read, 1)

            def negate_maxima(b, q):
                dve.wait_ge(rows_read, per_quarter(len(M_STEPS), b, q, len(M_STEPS)))
                link(nc.vector.tensor_reduce(neg_max[:, :], chunk_max[:, :, :], AX.X, ALU.max))
                nc.vector.tensor_scalar(neg_max[:, :], neg_max[:, :], -1.0, None, ALU.mult).then_inc(max_negated, 1)

            def split_maxima(b, q):
                dve.wait_ge(max_turned, per_quarter(1, b, q, 1))
                wait(dve, att_ready, per_quarter(1, b, q - 1, 0))
                turned = rows_ps[0:4, 0, :]
                link(nc.vector.tensor_copy(shift_parts[:, 0, :], turned))
                link(nc.vector.tensor_tensor(shift_rest, turned, shift_parts[:, 0, :], ALU.subtract))
                link(nc.vector.tensor_copy(shift_parts[:, 1, :], shift_rest))
                nc.vector.tensor_tensor(shift_parts[:, 2, :], shift_rest, shift_parts[:, 1, :],
                                        ALU.subtract).then_inc(shift_split, 1)

            def prologue():
                ones = denom[:, 0:P]
                nc.vector.memset(ones, 1.0).then_inc(setup_done, 1)
                dve.wait_ge(loaded, 16 * N_LOADS)
                dve.wait_ge(setup_done, 3)
                for g in range(4):
                    nc.vector.tensor_scalar(probs[:, 0, P * g:P * (g + 1)], ones, bv_pad[:, g:g + 1], None,
                                            ALU.mult).then_inc(bv_spread, 1)
                dve.wait_ge(bo_product, 1)
                nc.vector.tensor_tensor(bo_row[:, :], o_ps[:, 0:D], bo_row[:, :], ALU.add).then_inc(bo_made, 1)
                normalise_x(0)
                for m in range(len(M_STEPS)):
                    read_rows(0, 0, m)
                negate_maxima(0, 0)
                split_maxima(0, 0)

            def quarter(b, q, start, steps):
                first, last = (isinstance(b, int) and b == n for n in (0, B - 1))
                bm, qm = (b, q + 1) if q < 3 else (b + 1, 0)
                for u in range(UNITS):
                    if 2 <= u <= 6 and not (first and q == 0):
                        if u == 2:
                            spread_denominators(*((b, q - 1) if q > 0 else (b - 1, 3)))
                        else:
                            invert_denominators(u - 3)
                    if not (last and q == 3):
                        for m in maxima_at(u):
                            read_rows(bm, qm, m)
                        if u == TURN_UNIT - 1:
                            negate_maxima(bm, qm)
                        if u == TURN_UNIT:
                            split_maxima(bm, qm)
                    for k, kind, arg in at(steps, u):
                        if kind == "k" and arg == 0 and q == 1:
                            normalise_x(b + 1)
                        side_step(b - 1, start, k, kind, arg)

            def epilogue(start):
                spread_denominators(B - 1, 3)
                for piece in range(QT):
                    invert_denominators(piece)
                for k, (_, kind, arg) in enumerate(EPILOGUE):
                    side_step(B - 1, start, k, kind, arg)

            walk(dve, prologue, quarter, epilogue, [(seq, DVE_SEQ_PER_BATCH)])

        @block.tensor
        def _(pe):
            def side_step(b, s, start, k, kind, arg, steps):
                wait(pe, side_read, step_value(start, k - 1))
                if kind == "ctx":
                    c, kc = arg
                    pe.wait_ge(ctx_landed[c % 2], b * 32 + 16 * (c // 2 + 1))
                    for t in tiles_in(c):
                        rows, j = keys_in(t), t - 4 * c
                        last = nc.tensor.transpose(side[:, P * j:P * j + rows],
                                                   ctx_nat[0:rows, c % 2, j, P * kc:P * (kc + 1)],
                                                   ident[0:rows, 0:rows])
                elif kind == "x":
                    pe.wait_ge(xn_ready, b + 1)
                    for t in range(QT):
                        last = nc.tensor.transpose(side[:, P * t:P * (t + 1)], x_nat[:, t, P * arg:P * (arg + 1)],
                                                   ident[:, :])
                elif kind == "k":
                    for kc in range(KC):
                        last = nc.tensor.matmul(side[:, 0:width(arg)], wk_sb[:, kc, P * s:P * (s + 1)],
                                                ctxT[:, kc, CHUNK * arg:CHUNK * arg + width(arg)],
                                                start=(kc == 0), stop=(kc == KC - 1))
                elif kind == "q":
                    for kc in range(KC):
                        last = nc.tensor.matmul(side[:, :], wq_sb[:, kc, P * s:P * (s + 1)], qnT[:, kc, :],
                                                start=(kc == 0), stop=(kc == KC - 1))
                elif kind == "v":
                    for t in tiles_in(arg):
                        rows, j = keys_in(t), t - 4 * arg
                        for kc in range(KC):
                            last = nc.tensor.matmul(side[0:rows, P * j:P * (j + 1)], ctxT[:, kc, P * t:P * t + rows],
                                                    wv_sb[:, kc, P * s:P * (s + 1)], start=(kc == 0), stop=(kc == KC - 1))
                elif kind == "wo":
                    pe.wait_ge(att_ready, b * 4 + 4)
                    for t in range(2):
                        for g in range(4):
                            q0 = QH * arg + P * t
                            last = nc.tensor.matmul(side[:, D * t:D * (t + 1)], attT[:, g, q0:q0 + P], wo_pad[:, g, :],
                                                    start=(g == 0), stop=(g == 3))
                elif kind == "h":
                    pe.wait_ge(h_ready, b * 2 + (arg + 1))
                    for kc in range(KC):
                        for t in range(2):
                            last = nc.tensor.transpose(side[:, QH * kc + P * t:QH * kc + P * (t + 1)],
                                                       h_nat[:, t, P * kc:P * (kc + 1)], ident[:, :])
                elif kind == "w1":
                    hf, m2 = arg
                    for half in range(2):
                        m = 2 * m2 + half
                        for kc in range(KC):
                            last = nc.tensor.matmul(side[:, QH * half:QH * (half + 1)], w1_sb[:, kc, P * m:P * (m + 1)],
                                                    hT[:, kc, :], start=(kc == 0), stop=(kc == KC - 1))
                else:
                    pe.wait_ge(silu_done, b * 8 + 4 * (arg + 1))
                    for t in range(2):
                        for m in range(FM):
                            last = nc.tensor.matmul(side[:, D * t:D * (t + 1)], ffT[:, m, P * t:P * (t + 1)],
                                                    w2_sb[:, m, :], start=(m == 0), stop=(m == FM - 1))
                last.then_inc(side_ready, 1)

            def make_rows(b, q, m):
                r, c = M_STEPS[m]
                s = q // 2
                if m == 0:
                    pe.wait_ge(placed[s], (b + 1) * (16 * PLACED))
                    pe.wait_ge(stack_landed[s], (b + 1) * (16 * REPEATED))
                wait(pe, rows_read, per_quarter(len(M_STEPS), b, q, m - 1))
                for row in [r] if c is not None else range(r - 3, r + 1):
                    t, h = row // 4, 4 * (q % 2) + row % 4
                    k0, w, d0 = (CHUNK * c, CHUNK, 0) if c is not None else (CHUNK * (NCH - 1), TAIL, TAIL * (row - r + 3))
                    last = nc.tensor.matmul(rows_ps[:, m % 2, d0:d0 + w], q_stack[s][0:STACK, h, P * t:P * (t + 1)],
                                            k_stack[s][0:STACK, h, k0:k0 + w], start=True, stop=True)
                last.then_inc(rows_ready, 1)

            def turn_maxima(b, q):
                pe.wait_ge(max_negated, per_quarter(1, b, q, 1))
                for t in range(QT):
                    last = nc.tensor.transpose(rows_ps[0:4, 0, P * t:P * (t + 1)], neg_max[:, 4 * t:4 * t + 4], ident[:, :])
                last.then_inc(max_turned, 1)

            def make_scores(b, q, u):
                t, pair, s = u // 2, u % 2, q // 2
                if u == 0:
                    pe.wait_ge(shift_landed, per_quarter(16 * PARTS, b, q, 16 * PARTS))
                wait(pe, exp_done, per_quarter(UNITS, b, q, u - 1))
                for j in (2 * pair, 2 * pair + 1):
                    h = 4 * (q % 2) + j
                    last = nc.tensor.matmul(scores[0:keys_in(t), LQ * j:LQ * (j + 1)],
                                            k_stack[s][:, h, P * t:P * t + keys_in(t)], q_stack[s][:, h, :],
                                            start=True, stop=True)
                last.then_inc(scores_ready, 1)

            def multiply_v(b, q, t):
                pe.wait_ge(exp_done, per_quarter(UNITS, b, q, 2 * t + 2))
                if t == 0:
                    wait(pe, o_copied, per_quarter(1, b, q, 0))
                rows = keys_in(t)
                for j in range(4):
                    col = VH * (4 * (q % 2) + j)
                    last = nc.tensor.matmul(o_ps[32 * j:32 * j + 32, :], v_sb[q // 2][0:rows, t, col:col + 32],
                                            probs[0:rows, (q + t) % 2, LQ * j:LQ * (j + 1)],
                                            start=(t == 0), stop=(t == KT - 1))
                last.then_inc(pv_done, 1)

            def prologue():
                pe.wait_ge(ident_made, 2)
                pe.wait_ge(ones_set, 4)
                pe.wait_ge(loaded, 16 * N_LOADS)
                pe.wait_ge(bv_spread, 4)
                for g in range(4):
                    last = nc.tensor.matmul(o_ps[:, 0:D], probs[:, 0, P * g:P * (g + 1)], wo_pad[:, g, :],
                                            start=(g == 0), stop=(g == 3))
                last.then_inc(bo_product, 1)
                pe.wait_ge(bo_made, 1)
                n = 0
                for q in (1, 2, 3):
                    for k, (_, kind, arg) in enumerate(PREPARE[q]):
                        side_step(0, PREPARED[q][1], (0, n), k, kind, arg, PREPARE[q])
                    n += len(PREPARE[q])
                for m in range(len(M_STEPS)):
                    make_rows(0, 0, m)
                turn_maxima(0, 0)

            def quarter(b, q, start, steps):
                first, last = (isinstance(b, int) and b == n for n in (0, B - 1))
                bm, qm = (b, q + 1) if q < 3 else (b + 1, 0)
                ahead, s = PREPARED[q]
                for u in range(UNITS):
                    make_scores(b, q, u)
                    if u == 1 and not (first and q == 0):
                        multiply_v(*((b, q - 1) if q > 0 else (b - 1, 3)), KT - 1)
                    if u % 2 == 1 and u > 1:
                        multiply_v(b, q, u // 2 - 1)
                    if not (last and q == 3):
                        for m in maxima_at(u):
                            make_rows(bm, qm, m)
                        if u == TURN_UNIT:
                            turn_maxima(bm, qm)
                    for k, kind, arg in at(steps, u):
                        if kind in ("wo", "h", "w1", "w2"):
                            side_step(b - 1, None, start, k, kind, arg, steps)
                        else:
                            side_step(b + ahead, s, start, k, kind, arg, steps)

            def epilogue(start):
                multiply_v(B - 1, 3, KT - 1)
                for k, (_, kind, arg) in enumerate(EPILOGUE):
                    side_step(B - 1, None, start, k, kind, arg, EPILOGUE)

            walk(pe, prologue, quarter, epilogue)


_W = "L0_xattn_"
_INS = ["x", "ctx_1024", _W + "Wq", _W + "bq", _W + "Wk", _W + "bk", _W + "Wv", _W + "bv", _W + "Wo", _W + "bo",
        _W + "W1", _W + "b1", _W + "W2", _W + "b2", _W + "ln_q_g", _W + "ln_q_b", _W + "ln_ff_g", _W + "ln_ff_b"]


def kernel(**inputs):
    import numpy as np
    import concourse.bacc as bacc
    from concourse.bass_utils import run_bass_kernel_spmd

    nc = bacc.Bacc("TRN2", target_bir_lowering=False, num_devices=1)
    arrays, args = {}, []
    for name in _INS:
        a = np.ascontiguousarray(inputs[name])
        arrays[f"in_{name}"] = a
        args.append(nc.dram_tensor(f"in_{name}", a.shape, mybir.dt.from_np(a.dtype), kind="ExternalInput").ap())
    args.append(nc.dram_tensor("out", (B, LQ, D), F32, kind="ExternalOutput").ap())
    xattn_kernel(nc, *args)
    return run_bass_kernel_spmd(nc, [arrays], core_ids=[0]).results[0]["out"]
```

```python
from contextlib import ExitStack

import concourse.bass as bass
from concourse import mybir

F32 = mybir.dt.float32
BF16 = mybir.dt.bfloat16
I32 = mybir.dt.int32
ACT = mybir.ActivationFunctionType
ALU = mybir.AluOpType
AX = mybir.AxisListType

P = 128
B, LQ, D = 16, 512, 256
LK = 1601
H, DH = 16, 16
FF = 1024
EPS = 1e-5
KC = D // P
FM = FF // P
KT = (LK + P - 1) // P
LAST = LK - (KT - 1) * P
CHUNK = 512
NCH = (LK + CHUNK - 1) // CHUNK
QT = LQ // P
HH = H // 2
UNITS = KT * 2
PARTS = 3
K_ROWS = (0, 0, 0, 1, 1, 2)
Q_ROWS = (0, 1, 2, 0, 1, 0)
STACK = 16 * len(K_ROWS)
ROWS = STACK + PARTS
VH = DH + 1
VW = VH * (HH - 1) + 32
QH = LQ // 2
PLACED = 2 * 4 * PARTS
REPEATED = 2 * (len(K_ROWS) - PARTS)
N_LOADS = 5 + 7 + 2 + 8


def keys_in(t):
    return P if t < KT - 1 else LAST


def width(c):
    return min(CHUNK, LK - c * CHUNK)


def tiles_in(c):
    return range(4 * c, min(4 * c + 4, KT))


PREPARE = (
    [(0, 1, "v", 0), (2, 3, "v", 1), (4, 5, "v", 2), (11, 11, "v", 3)],
    [(u, u, "ctx", (n // KC, n % KC)) for n, u in enumerate((0, 1, 2, 3, 5, 6, 7, 8))]
    + [(12, 13, "k", 0), (14, 15, "k", 1), (16, 17, "k", 2), (18, 18, "k", 3), (19, 19, "x", 0), (20, 20, "x", 1),
       (24, 24, "q", 0)],
    [(0, 1, "v", 0), (2, 3, "v", 1), (4, 5, "v", 2), (6, 6, "v", 3)],
    [(0, 1, "k", 0), (2, 3, "k", 1), (4, 5, "k", 2), (6, 6, "k", 3), (8, 9, "q", 0)],
)
PREPARED = ((0, 1), (1, 0), (1, 0), (1, 1))
FINISH = (
    [(7, 9, "wo", 0), (18, 18, "h", 0), (20, 21, "wo", 1), (24, 24, "w1", (0, 0))],
    [(10, 10, "w1", (0, 1))],
    [(8, 8, "w1", (0, 2)), (10, 10, "w1", (0, 3)), (13, 15, "w2", 0), (17, 17, "h", 1), (18, 19, "w1", (1, 0)),
     (20, 21, "w1", (1, 1))],
    [(11, 12, "w1", (1, 2)), (14, 15, "w1", (1, 3)), (18, 20, "w2", 1)],
)
TURN = [(22, 22, "turn", 0)]


def in_order(*lists):
    return sorted(sum(lists, []), key=lambda step: step[:2])


FIRST = tuple(in_order(p, TURN) for p in PREPARE)
BOTH = tuple(in_order(p, f, TURN) for p, f in zip(PREPARE, FINISH))
LAST_BATCH = (BOTH[0],) + tuple(in_order(f, TURN) for f in FINISH[1:3]) + (FINISH[3],)
PER_BATCH = sum(map(len, BOTH))
BEFORE = sum(len(PREPARE[q]) for q in (1, 2, 3)) + 1
LATER = BEFORE + sum(map(len, FIRST)) - PER_BATCH
EPILOGUE = FINISH[0] + FINISH[1] + FINISH[2] + FINISH[3]


def starts(first, quarters):
    return [first + sum(map(len, quarters[:q])) for q in range(4)]


def at(steps, u):
    return [(n, kind, arg) for n, (_, last, kind, arg) in enumerate(steps) if last == u]


def index(steps, kind, arg):
    return [step[2:] for step in steps].index((kind, arg))


def products(kind, arg):
    if kind in ("v", "ctx"):
        c = arg if kind == "v" else arg[0]
        return [(t, kc) for t in tiles_in(c) for kc in (range(KC) if kind == "v" else [arg[1]])]
    first, second = {"turn": (QT, 1), "x": (QT, 1), "k": (1, KC), "q": (1, KC), "wo": (2, 4), "h": (KC, 2), "w1": (2, KC), "w2": (2, FM)}[kind]
    return [(i, j) for i in range(first) for j in range(second)]


def products_at(steps, u):
    found = []
    for n, (first, last, kind, arg) in enumerate(steps):
        todo, units = products(kind, arg), last - first + 1
        for k, product in enumerate(todo):
            if first + k * units // len(todo) == u:
                found.append((n, kind, arg, product, k, k == len(todo) - 1))
    return found


M_ROWS = QT * 4
TAIL = width(NCH - 1)
M_STEPS = [step for r in range(M_ROWS) for step in [(r, c) for c in range(NCH - 1)] + [(r, None)] * (r % 4 == 3)]
PER_TILE = len(M_STEPS) // KT
assert PER_TILE * KT == len(M_STEPS) and len(M_STEPS) % 2 == 0
M_END = 20
OWN = M_END // 2 * PER_TILE
EARLY = len(M_STEPS) - OWN
MAX_PHASE = 0.5
FIRST_MAXIMA = 26
STAGES = 3
X_UNIT = 4


def maxima(b, q, slot):
    ahead, m = (1, EARLY + slot) if slot < OWN else (2, slot - OWN)
    if isinstance(b, int) and b == B - 1 and q + ahead >= 4:
        return None
    return b + (q + ahead) // 4, (q + ahead) % 4, m


COST = {"scores": 512, "pv": 2048, "v": 512, "ctx": 256, "x": 256, "h": 256, "turn": 128, "k": 2048, "q": 2048,
        "wo": 1024, "w1": 1024, "w2": 1024}


def plan(steps):
    units, slot = [], 0
    for t in range(KT):
        work = []
        for u in (2 * t, 2 * t + 1):
            work += [(u, "scores", j) for j in range(2)]
            work += [(u, "side", product) for product in products_at(steps, u)]
            work += [(u, "pv", None)] * (u % 2)
        costs = [COST[what[1] if kind == "side" else kind] for _, kind, what in work]
        done, placed, tile = 0, 0, {2 * t: [], 2 * t + 1: []}
        for (u, kind, what), cost in zip(work, costs):
            tile[u].append((kind, what))
            done += cost
            while placed < PER_TILE and done * PER_TILE >= (placed + MAX_PHASE) * sum(costs):
                tile[u].append(("max", slot))
                placed, slot = placed + 1, slot + 1
        units += [tile[2 * t], tile[2 * t + 1]]
    return units


def wait(eng, sem, value):
    if not (isinstance(value, int) and value <= 0):
        eng.wait_ge(sem, value)


class Tally:

    def __init__(self, sem):
        self.sem, self.start, self.here, self.loop = sem, 0, 0, None

    def inc(self, ins):
        self.here += 1
        ins.then_inc(self.sem, 1)

    @property
    def value(self):
        if self.loop is None:
            return self.start + self.here
        i, per = self.loop
        return i * per + (self.start - per + self.here)

    def enter(self, i, per):
        self.start, self.here, self.loop = self.start + self.here, 0, (i, per)

    def leave(self, rounds):
        assert self.here == self.loop[1], f"a round counts {self.here}"
        self.start, self.here, self.loop = self.start + self.here * rounds, 0, None


DVE_SEQ_PER_BATCH = 54
POOL_SEQ_PER_BATCH = 56


def xattn_kernel(nc, x, ctx, wq, bq, wk, bk, wv, bv, wo, bo, w1, b1, w2, b2, gq, cq, gf, cf, out):
    with ExitStack() as stack:
        def sb(name, shape, dt=F32):
            return stack.enter_context(nc.sbuf_tensor(name, shape, dt))

        def sem(name):
            return stack.enter_context(nc.semaphore(name))

        ident = sb("ident", [P, P])
        wq_sb = sb("wq_sb", [P, KC, D])
        wk_sb = sb("wk_sb", [P, KC, D])
        wv_sb = sb("wv_sb", [P, KC, D])
        wo_pad = sb("wo_pad", [P, 4, D])
        w1_sb = sb("w1_sb", [P, KC, FF])
        w2_sb = sb("w2_sb", [P, FM, D])
        bq_c = sb("bq_c", [P, KC])
        bk_c = sb("bk_c", [P, KC])
        bv_pad = sb("bv_pad", [P, 4])
        b1_c = sb("b1_c", [P, FM])
        half_b1 = sb("half_b1", [P, FM])
        gq_c, cq_c, gf_c, cf_c = (sb(n, [P, KC]) for n in ("gq_c", "cq_c", "gf_c", "cf_c"))
        bo_row = sb("bo_row", [P, D])
        b2_row = sb("b2_row", [P, D])
        ctx_nat = sb("ctx_nat", [P, 2, 4, D])
        ctxT = sb("ctxT", [P, KC, LK])
        x_nat = sb("x_nat", [P, QT, D])
        qnT = sb("qnT", [P, KC, LQ])
        whole = sb("whole", [P, 2, CHUNK])
        rest = sb("rest", [P, CHUNK])
        k_parts = sb("k_parts", [P, PARTS, LK], BF16)
        q_parts = sb("q_parts", [P, PARTS, LQ], BF16)
        k_stack = [sb(f"k_stack{s}", [ROWS, HH, LK], BF16) for s in range(2)]
        q_stack = [sb(f"q_stack{s}", [ROWS, HH, LQ], BF16) for s in range(2)]
        v_sb = [sb(f"v_sb{s}", [P, KT, VW]) for s in range(2)]
        chunk_max = sb("chunk_max", [P, M_ROWS, NCH])
        neg_max = sb("neg_max", [P, QT, 4])
        neg_parts = sb("neg_parts", [P, QT, PARTS, 4], BF16)
        shift_parts = sb("shift_parts", [PARTS * 4, LQ], BF16)
        ident_bf = sb("ident_bf", [P, P], BF16)
        probs = sb("probs", [P, 2, 4 * LQ])
        o_sb = sb("o_sb", [P, LQ])
        denom = sb("denom", [P, LQ])
        inverse = sb("inverse", [P, LQ // 32])
        attT = sb("attT", [P, 4, LQ])
        stats = sb("stats", [P, QT, 6])
        moments = sb("moments", [P, QT, 2])
        rstd, half_var, newton = (sb(n, [P, QT]) for n in ("rstd", "half_var", "newton"))
        resid = [sb(f"resid{i}", [P, 2, D]) for i in range(2)]
        h_nat = sb("h_nat", [P, 2, D])
        hT = sb("hT", [P, KC, QH])
        tanh_sb = sb("tanh_sb", [P, 2 * QH])
        ffT = sb("ffT", [P, FM, QH])

        scores = stack.enter_context(nc.psum_tensor("scores", [P, 4 * LQ], F32))
        o_ps = stack.enter_context(nc.psum_tensor("o_ps", [P, LQ], F32))
        side = stack.enter_context(nc.psum_tensor("side", [P, CHUNK], F32))
        rows_ps = stack.enter_context(nc.psum_tensor("rows_ps", [P, 2, CHUNK], F32))

        loaded = sem("loaded")
        zeroed = sem("zeroed")
        ident_made = sem("ident_made")
        bv_spread = sem("bv_spread")
        bo_product = sem("bo_product")
        bo_made = sem("bo_made")
        setup_done = sem("setup_done")
        ones_set = sem("ones_set")
        ctx_landed = [sem(f"ctx_landed{i}") for i in range(2)]
        x_landed = sem("x_landed")
        x_guessed = sem("x_guessed")
        h_guessed = sem("h_guessed")
        xn_ready = sem("xn_ready")
        side_ready = sem("side_ready")
        side_read = sem("side_read")
        split = sem("split")
        pool_seq = sem("pool_seq")
        placed = [sem(f"placed{g}") for g in range(4)]
        stack_landed = [sem(f"stack_landed{g}") for g in range(4)]
        scores_ready = sem("scores_ready")
        exp_done = sem("exp_done")
        pv_done = sem("pv_done")
        o_copied = sem("o_copied")
        inverted = sem("inverted")
        att_ready = sem("att_ready")
        rows_ready = sem("rows_ready")
        rows_read = sem("rows_read")
        max_negated = sem("max_negated")
        shift_landed = sem("shift_landed")
        resid_landed = [sem(f"resid_landed{i}") for i in range(2)]
        resid_ready = sem("resid_ready")
        h_ready = sem("h_ready")
        mlp_biased = sem("mlp_biased")
        silu_done = sem("silu_done")
        y_stored = [sem(f"y_stored{i}") for i in range(2)]
        dve_seq = sem("dve_seq")
        passed = sem("passed")

        def wait_apart(eng, sem, value):
            wait(eng, sem, value)
            if not isinstance(value, int):
                eng.sem_inc(passed, 1)

        def step_value(start, k):
            b, c = start
            return b * PER_BATCH + (c + k + 1)

        def per_quarter(n, b, q, more):
            return b * (4 * n) + (n * q + more)

        def walk(eng, prologue, quarter, epilogue, tallies=()):
            prologue()
            for q, c in enumerate(starts(BEFORE, FIRST)):
                quarter(0, q, (0, c), FIRST[q])
            with eng.Fori(1, B - 1) as b:
                for tally, per in tallies:
                    tally.enter(b, per)
                for q, c in enumerate(starts(LATER, BOTH)):
                    quarter(b, q, (b, c), BOTH[q])
                for tally, _ in tallies:
                    tally.leave(B - 2)
            for q, c in enumerate(starts(LATER, LAST_BATCH)):
                quarter(B - 1, q, (B - 1, c), LAST_BATCH[q])
            epilogue((B - 1, LATER + sum(map(len, LAST_BATCH))))

        block = stack.enter_context(nc.Block())

        @block.sync
        def _(sp):
            def column(dst, src, n):
                with nc.allow_non_contiguous_dma(reason="a bias, once"):
                    sp.dma_start(dst[:, 0:n], src.rearrange("(c p) -> p c", p=P)).then_inc(loaded, 16)

            def load_ctx(b, c):
                if c < NCH - 1:
                    src = ctx[b, CHUNK * c:CHUNK * (c + 1), :].rearrange("(t p) d -> p t d", p=P)
                    sp.dma_start(ctx_nat[:, c % 2, :, :], src).then_inc(ctx_landed[c % 2], 16)
                else:
                    sp.dma_start(ctx_nat[0:LAST, c % 2, 0, :], ctx[b, CHUNK * c:LK, :]).then_inc(ctx_landed[c % 2], 16)

            def load_x(b):
                sp.dma_start(x_nat[:, :, :], x[b].rearrange("(t p) d -> p t d", p=P)).then_inc(x_landed, 16)

            def load_resid(b, hf):
                wait_apart(sp, y_stored[hf], b * 16)
                sp.dma_start(resid[hf][:, :, :], x[b, QH * hf:QH * (hf + 1), :].rearrange("(t p) d -> p t d", p=P))\
                    .then_inc(resid_landed[hf], 16)

            def place(dst, src, rows, g):
                for part in range(PARTS):
                    slot = rows.index(part)
                    for h in range(4 * (g % 2), 4 * (g % 2) + 4):
                        sp.dma_start(dst[16 * slot:16 * slot + 16, h, :], src[16 * h:16 * h + 16, part, :])\
                            .then_inc(placed[g], 16)

            def repeat(b, g):
                wait_apart(sp, placed[g], (b + 1) * (16 * PLACED))
                heads = slice(4 * (g % 2), 4 * (g % 2) + 4)
                for dst, rows in ((k_stack[g // 2], K_ROWS), (q_stack[g // 2], Q_ROWS)):
                    for slot, part in enumerate(rows):
                        first = rows.index(part)
                        if slot != first:
                            sp.dma_start(dst[16 * slot:16 * slot + 16, heads, :],
                                         dst[16 * first:16 * first + 16, heads, :]).then_inc(stack_landed[g], 16)

            def fill_stacks(b, s):
                wait_apart(sp, scores_ready, per_quarter(UNITS, b, 2 * s - 2, 0))
                wait_apart(sp, split, b * 10 + (5 * s + 4))
                place(k_stack[s], k_parts, K_ROWS, 2 * s)
                wait_apart(sp, split, b * 10 + (5 * s + 5))
                place(q_stack[s], q_parts, Q_ROWS, 2 * s)
                place(k_stack[s], k_parts, K_ROWS, 2 * s + 1)
                repeat(b, 2 * s)
                place(q_stack[s], q_parts, Q_ROWS, 2 * s + 1)
                repeat(b, 2 * s + 1)

            def place_shift(q, start, k):
                wait_apart(sp, side_read, step_value(start, k))
                g = q % 2
                for i in range(PARTS):
                    sp.dma_start(q_stack[q // 2][STACK + i:STACK + i + 1, 4 * g:4 * g + 4, :],
                                 shift_parts[4 * i:4 * i + 4, :])\
                        .then_inc(shift_landed, 16)

            def store_y(b, hf, start, k):
                wait_apart(sp, side_read, step_value(start, k))
                sp.dma_start(out[b, QH * hf:QH * (hf + 1), :].rearrange("(t p) d -> p t d", p=P), resid[hf][:, :, :])\
                    .then_inc(y_stored[hf], 16)

            def prologue():
                sp.dma_start(wk_sb[:, :, :], wk.rearrange("(c p) n -> p c n", p=P)).then_inc(loaded, 16)
                load_ctx(0, 0)
                load_ctx(0, 1)
                load_x(0)
                for dst, src in ((wq_sb, wq), (wv_sb, wv), (w1_sb, w1), (w2_sb, w2)):
                    sp.dma_start(dst[:, :, :], src.rearrange("(c p) n -> p c n", p=P)).then_inc(loaded, 16)
                for dst, src, n in ((bq_c, bq, KC), (bk_c, bk, KC), (b1_c, b1, FM), (gq_c, gq, KC), (cq_c, cq, KC),
                                    (gf_c, gf, KC), (cf_c, cf, KC)):
                    column(dst, src, n)
                for dst, src in ((bo_row, bo), (b2_row, b2)):
                    sp.dma_start(dst[:, :], src.partition_broadcast(P)).then_inc(loaded, 16)
                sp.wait_ge(zeroed, 2)
                for j in range(4):
                    rows = wo.rearrange("(g j d) n -> j d g n", g=4, j=4)[j]
                    sp.dma_start(wo_pad[32 * j:32 * j + 16, :, :], rows).then_inc(loaded, 16)
                    with nc.allow_non_contiguous_dma(reason="a bias, once"):
                        sp.dma_start(bv_pad[32 * j:32 * j + 16, :], bv.rearrange("(g j d) -> j d g", g=4, j=4)[j])\
                            .then_inc(loaded, 16)
                for c in (2, 3):
                    sp.wait_ge(side_ready, index(PREPARE[1], "ctx", (c - 2, KC - 1)) + 1)
                    load_ctx(0, c)
                fill_stacks(0, 0)
                place_shift(0, (0, BEFORE - 1), 0)

            def quarter(b, q, start, steps):
                last = isinstance(b, int) and b == B - 1
                kinds = [step[2:] for step in steps]
                if q == 0:
                    if not (isinstance(b, int) and b == 0):
                        load_resid(b - 1, 1)
                    fill_stacks(b, 1)
                if q == 1 and not last:
                    load_ctx(b + 1, 0)
                    load_ctx(b + 1, 1)
                    load_x(b + 1)
                    for c in (2, 3):
                        wait_apart(sp, side_ready, step_value(start, kinds.index(("ctx", (c - 2, KC - 1)))))
                        load_ctx(b + 1, c)
                if q == 2:
                    if not last:
                        fill_stacks(b + 1, 0)
                    if ("w2", 0) in kinds:
                        store_y(b - 1, 0, start, kinds.index(("w2", 0)))
                if q == 3:
                    load_resid(b, 0)
                    if ("w2", 1) in kinds:
                        store_y(b - 1, 1, start, kinds.index(("w2", 1)))
                if ("turn", 0) in kinds:
                    place_shift((q + 1) % 4, start, kinds.index(("turn", 0)))

            def epilogue(start):
                load_resid(B - 1, 1)
                for hf in range(2):
                    store_y(B - 1, hf, start, index(EPILOGUE, "w2", hf))
                for hf in range(2):
                    sp.wait_ge(y_stored[hf], 16 * B)

            walk(sp, prologue, quarter, epilogue)

        @block.gpsimd
        def _(pool):
            seq = Tally(pool_seq)

            def read_parts(b, s, start, k, use):
                n, w = 5 * s + use, width(use) if use < NCH else LQ
                parts, off = (k_parts, CHUNK * use) if use < NCH else (q_parts, 0)
                src, first, second = whole[:, n % 2, 0:w], parts[:, 0, off:off + w], parts[:, 1, off:off + w]
                pool.wait_ge(side_read, step_value(start, k))
                wait(pool, split, b * 10 + n)
                seq.inc(nc.gpsimd.tensor_tensor(rest[:, 0:w], src, first, ALU.subtract))
                seq.inc(nc.gpsimd.tensor_tensor(second, src, first, ALU.subtract))
                pool.wait_ge(pool_seq, seq.value)
                nc.gpsimd.tensor_tensor(parts[:, 2, off:off + w], rest[:, 0:w], second, ALU.subtract).then_inc(split, 1)

            def follow(ins):
                seq.inc(ins)
                wait_apart(pool, pool_seq, seq.value)

            def normalise(src, dst, tiles, ready):
                y, v, t = rstd[:, 0:tiles], half_var[:, 0:tiles], newton[:, 0:tiles]
                for _ in range(3):
                    follow(nc.gpsimd.tensor_tensor(t, y, y, ALU.mult))
                    follow(nc.gpsimd.tensor_tensor(t, t, v, ALU.mult))
                    follow(nc.gpsimd.tensor_scalar(t, t, 1.5, None, ALU.add))
                    follow(nc.gpsimd.tensor_tensor(y, y, t, ALU.mult))
                for n in range(tiles):
                    last = nc.gpsimd.tensor_scalar(dst[:, n, :], src[:, n, :], moments[:, n, 0:1], rstd[:, n:n + 1],
                                                   ALU.subtract, ALU.mult)
                last.then_inc(ready, 1)

            def normalise_x(b):
                pool.wait_ge(x_guessed, b + 1)
                normalise(x_nat, x_nat, QT, xn_ready)

            def normalise_sum(b, hf):
                pool.wait_ge(h_guessed, b * 2 + (hf + 1))
                normalise(resid[hf], h_nat, 2, h_ready)

            def add_output_bias(b, hf):
                pool.wait_ge(resid_landed[hf], b * 16 + 16)
                nc.gpsimd.tensor_tensor(resid[hf][:, :, :], resid[hf][:, :, :],
                                        bo_row[:, :].unsqueeze(1).broadcast_to((P, 2, D)),
                                        ALU.add).then_inc(resid_ready, 1)

            def add_mlp_bias(b, hf):
                pool.wait_ge(h_ready, b * 2 + (hf + 1))
                nc.gpsimd.tensor_tensor(resid[hf][:, :, :], resid[hf][:, :, :],
                                        b2_row[:, :].unsqueeze(1).broadcast_to((P, 2, D)),
                                        ALU.add).then_inc(mlp_biased, 1)

            def scale_group(b, q):
                pool.wait_ge(inverted, per_quarter(1, b, q, 1))
                nc.gpsimd.tensor_tensor(attT[:, q, :], o_sb[:, :], denom[:, :], ALU.mult).then_inc(att_ready, 1)

            def splits(b, s, start, steps):
                for k, (_, _, kind, arg) in enumerate(steps):
                    if kind in ("k", "q"):
                        read_parts(b, s, start, k, arg if kind == "k" else NCH)

            def prologue():
                pool.memset(wo_pad[:, :, :], 0.0).then_inc(zeroed, 1)
                pool.memset(bv_pad[:, :], 0.0).then_inc(zeroed, 1)
                pool.memset(ident[:, :], 0.0).then_inc(ident_made, 1)
                pool.wait_ge(ident_made, 1)
                pool.affine_select(out=ident[:, :], in_=ident[:, :], compare_op=ALU.not_equal, fill=1.0, base=0,
                                   pattern=[[-1, P]], channel_multiplier=1).then_inc(ident_made, 1)
                pool.wait_ge(ident_made, 2)
                pool.tensor_copy(ident_bf[:, :], ident[:, :]).then_inc(ident_made, 1)
                for s in range(2):
                    pool.memset(v_sb[s][:, :, :], 1.0).then_inc(ones_set, 1)
                pool.wait_ge(bo_made, 1)
                pool.wait_ge(loaded, 16 * N_LOADS)
                normalise_x(0)
                n = 0
                for q, (_, s) in ((1, PREPARED[1]), (2, PREPARED[2]), (3, PREPARED[3])):
                    splits(0, s, (0, n), PREPARE[q])
                    n += len(PREPARE[q])

            def quarter(b, q, start, steps):
                kinds = [step[2:] for step in steps]
                ahead, s = PREPARED[q]
                if q == 3:
                    splits(b + ahead, s, start, steps)
                if q > 0:
                    scale_group(b, q - 1)
                elif not (isinstance(b, int) and b == 0):
                    scale_group(b - 1, 3)
                if ("wo", 0) in kinds:
                    for hf in range(2):
                        add_output_bias(b - 1, hf)
                    for hf in range(2):
                        normalise_sum(b - 1, hf)
                        add_mlp_bias(b - 1, hf)
                if ("x", 0) in kinds:
                    normalise_x(b + 1)
                if q != 3:
                    splits(b + ahead, s, start, steps)

            def epilogue(start):
                scale_group(B - 1, 3)
                for hf in range(2):
                    add_output_bias(B - 1, hf)
                for hf in range(2):
                    normalise_sum(B - 1, hf)
                    add_mlp_bias(B - 1, hf)

            walk(pool, prologue, quarter, epilogue, [(seq, POOL_SEQ_PER_BATCH)])

        @block.scalar
        def _(act):
            def side_step(b, s, start, k, kind, arg):
                if kind in ("wo", "w2"):
                    return
                act.wait_ge(side_ready, step_value(start, k))
                if kind == "ctx":
                    c, kc = arg
                    last = nc.scalar.copy(ctxT[:, kc, CHUNK * c:CHUNK * c + width(c)], side[:, 0:width(c)])
                elif kind == "turn":
                    last = nc.scalar.copy(shift_parts[:, :], side[0:4 * PARTS, :])
                elif kind == "x":
                    last = nc.scalar.activation(qnT[:, arg, :], side[:, :], ACT.Identity, bias=cq_c[:, arg:arg + 1],
                                                scale=gq_c[:, arg:arg + 1])
                elif kind == "h":
                    for kc in range(KC):
                        last = nc.scalar.activation(hT[:, kc, :], side[:, QH * kc:QH * (kc + 1)], ACT.Identity,
                                                    bias=cf_c[:, kc:kc + 1], scale=gf_c[:, kc:kc + 1])
                elif kind == "v":
                    if arg == 0:
                        wait(act, pv_done, per_quarter(KT, b, 2 * s - 2, 0))
                    tiles, rows = tiles_in(arg), keys_in(tiles_in(arg)[-1])
                    dst = v_sb[s][0:rows, tiles[0]:tiles[-1] + 1, 0:VH * HH].rearrange("p t (h e) -> p t h e", e=VH)
                    last = nc.scalar.copy(dst[:, :, :, 0:DH], side[0:rows, 0:P * len(tiles)].rearrange(
                        "p (t h e) -> p t h e", t=len(tiles), e=DH))
                elif kind in ("k", "q"):
                    use = arg if kind == "k" else NCH
                    n, w = 5 * s + use, width(use) if use < NCH else LQ
                    parts, off = (k_parts, CHUNK * use) if kind == "k" else (q_parts, 0)
                    bias, scale = (bk_c[:, s:s + 1], 1.0) if kind == "k" else (bq_c[:, s:s + 1], 1.0 / DH ** 0.5)
                    if kind == "k" and arg == 0:
                        for g in (2 - 2 * s, 3 - 2 * s):
                            wait(act, placed[g], (b + s) * (16 * PLACED))
                    wait(act, split, b * 10 + (n - 1))
                    nc.scalar.activation(whole[:, n % 2, 0:w], side[:, 0:w], ACT.Identity, bias=bias, scale=scale)
                    last = nc.scalar.activation(parts[:, 0, off:off + w], side[:, 0:w], ACT.Identity, bias=bias,
                                                scale=scale)
                else:
                    hf, m2 = arg
                    if m2 > 0:
                        act.wait_ge(silu_done, b * 8 + (4 * hf + m2))
                    for half in range(2):
                        m = 2 * m2 + half
                        cols = slice(QH * half, QH * (half + 1))
                        nc.scalar.activation(ffT[:, m, :], side[:, cols], ACT.Identity, bias=half_b1[:, m:m + 1],
                                             scale=0.5)
                        last = nc.scalar.activation(tanh_sb[:, cols], side[:, cols], ACT.Tanh,
                                                    bias=half_b1[:, m:m + 1], scale=0.5)
                last.then_inc(side_read, 1)

            def copy_group(b, q):
                act.wait_ge(pv_done, per_quarter(KT, b, q, KT))
                wait(act, att_ready, per_quarter(1, b, q, 0))
                nc.scalar.copy(o_sb[:, :], o_ps[:, :]).then_inc(o_copied, 1)

            def prologue():
                n = 0
                for q in (1, 2, 3):
                    for k, (_, _, kind, arg) in enumerate(PREPARE[q]):
                        if (q, kind, arg) == (1, "k", 0):
                            act.wait_ge(loaded, 16 * N_LOADS)
                            nc.scalar.mul(bq_c[:, :], bq_c[:, :], 1.0 / DH ** 0.5).then_inc(setup_done, 1)
                            nc.scalar.mul(half_b1[:, :], b1_c[:, :], 0.5).then_inc(setup_done, 1)
                            act.wait_ge(setup_done, 3)
                            act.wait_ge(ones_set, 4)
                        side_step(0, PREPARED[q][1], (0, n), k, kind, arg)
                    n += len(PREPARE[q])
                side_step(0, 0, (0, n), 0, "turn", 0)

            def quarter(b, q, start, steps):
                ahead, s = PREPARED[q]
                for u in range(UNITS):
                    t, pair = u // 2, u % 2
                    rows = keys_in(t)
                    if u == 2:
                        if q > 0:
                            copy_group(b, q - 1)
                        elif not (isinstance(b, int) and b == 0):
                            copy_group(b - 1, 3)
                    act.wait_ge(scores_ready, per_quarter(UNITS, b, q, u + 1))
                    if pair == 0:
                        wait(act, pv_done, per_quarter(KT, b, q, t - 1))
                    nc.scalar.activation(probs[0:rows, (q + t) % 2, 2 * LQ * pair:2 * LQ * (pair + 1)],
                                         scores[0:rows, 2 * LQ * pair:2 * LQ * (pair + 1)], ACT.Exp)\
                        .then_inc(exp_done, 1)
                    for k, kind, arg in at(steps, u):
                        if kind in ("h", "w1"):
                            side_step(b - 1, None, start, k, kind, arg)
                        else:
                            side_step(b + ahead, s, start, k, kind, arg)

            def epilogue(start):
                copy_group(B - 1, 3)
                for k, (_, _, kind, arg) in enumerate(EPILOGUE):
                    side_step(B - 1, None, start, k, kind, arg)

            walk(act, prologue, quarter, epilogue)

        @block.vector
        def _(dve):
            seq = Tally(dve_seq)

            def link(ins):
                seq.inc(ins)
                dve.wait_ge(dve_seq, seq.value)

            def take_moments(src, tiles, stage, guessed, free):
                y, v = rstd[:, 0:tiles], half_var[:, 0:tiles]
                if stage == 0:
                    for n in range(tiles):
                        seq.inc(nc.vector.bn_stats(stats[:, n, :], src[:, n, :]))
                elif stage == 1:
                    for semaphore, value in free:
                        wait_apart(dve, semaphore, value)
                    wait_apart(dve, dve_seq, seq.value)
                    for n in range(tiles):
                        seq.inc(nc.vector.bn_aggr(moments[:, n, :], stats[:, n, :]))
                else:
                    dve.wait_ge(dve_seq, seq.value)
                    link(nc.vector.tensor_scalar(v, moments[:, 0:tiles, 1], EPS, None, ALU.add))
                    link(nc.vector.tensor_scalar(y.bitcast(I32), v.bitcast(I32), -0.5, float(0x5F3759DF),
                                                 ALU.mult, ALU.add))
                    nc.vector.tensor_scalar(v, v, -0.5, None, ALU.mult).then_inc(guessed, 1)

            def add_step(b, start, k, kind, hf):
                dve.wait_ge(side_ready, step_value(start, k))
                if kind == "wo":
                    dve.wait_ge(resid_ready, b * 2 + (hf + 1))
                else:
                    dve.wait_ge(mlp_biased, b * 2 + (hf + 1))
                nc.vector.tensor_tensor(resid[hf][:, :, :], side[:, :].rearrange("p (t d) -> p t d", d=D),
                                        resid[hf][:, :, :], ALU.add).then_inc(side_read, 1)

            def sum_moments(b, start, k, hf, stage):
                if stage == 0:
                    dve.wait_ge(side_read, step_value(start, k))
                epilogue_half = isinstance(b, int) and b == B - 1 and hf == 0
                free = [(h_ready, b * 2 + hf)] if hf or epilogue_half else [(xn_ready, b + 2)]
                take_moments(resid[hf], 2, stage, h_guessed, free)

            def finish_silu(b, start, k, arg):
                hf, m2 = arg
                dve.wait_ge(side_read, step_value(start, k))
                z = ffT[:, 2 * m2:2 * m2 + 2, :].rearrange("p m q -> p (m q)")
                nc.vector.scalar_tensor_tensor(z, tanh_sb[:, :], 1.0, z, ALU.add, ALU.mult).then_inc(silu_done, 1)

            def x_moments(b, stage):
                if stage == 0:
                    dve.wait_ge(x_landed, b * 16 + 16)
                free = [] if isinstance(b, int) and b == 0 else \
                    [(xn_ready, 1)] if isinstance(b, int) and b == 1 else [(h_ready, (b - 1) * 2)]
                take_moments(x_nat, QT, stage, x_guessed, free)

            def invert_denominators(b, q, stage):
                blocks = denom[:, :].rearrange("p (c r) -> p c r", r=32)
                if stage == 0:
                    dve.wait_ge(o_copied, per_quarter(1, b, q, 1))
                    seq.inc(nc.vector.transpose(denom[:, :], o_sb[:, :]))
                else:
                    dve.wait_ge(dve_seq, seq.value)
                    link(nc.vector.reciprocal(inverse[:, :], blocks[:, :, DH]))
                    nc.vector.transpose(blocks, inverse[:, :].unsqueeze(2).broadcast_to((P, LQ // 32, 32)))\
                        .then_inc(inverted, 1)

            def read_rows(b, q, m):
                r, c = M_STEPS[m]
                dve.wait_ge(rows_ready, per_quarter(len(M_STEPS), b, q, m + 1))
                if c is None:
                    dst = chunk_max[:, r - 3:r + 1, NCH - 1]
                    src = rows_ps[:, m % 2, 0:4 * TAIL].rearrange("p (r k) -> p r k", k=TAIL)
                else:
                    dst, src = chunk_max[:, r, c:c + 1], rows_ps[:, m % 2, :]
                nc.vector.tensor_reduce(dst, src, AX.X, ALU.max).then_inc(rows_read, 1)

            def negate_maxima(b, q):
                dve.wait_ge(rows_read, per_quarter(len(M_STEPS), b, q, len(M_STEPS)))
                link(nc.vector.tensor_reduce(neg_max[:, :, :], chunk_max[:, :, :].rearrange("p (t h) c -> p t h c", h=4),
                                             AX.X, ALU.max))
                link(nc.vector.tensor_scalar(neg_max[:, :, :], neg_max[:, :, :], -1.0, None, ALU.mult))
                for part in range(PARTS - 1):
                    link(nc.vector.tensor_copy(neg_parts[:, :, part, :], neg_max[:, :, :]))
                    link(nc.vector.tensor_tensor(neg_max[:, :, :], neg_max[:, :, :], neg_parts[:, :, part, :],
                                                 ALU.subtract))
                nc.vector.tensor_copy(neg_parts[:, :, PARTS - 1, :], neg_max[:, :, :]).then_inc(max_negated, 1)

            def prologue():
                ones = denom[:, 0:P]
                nc.vector.memset(ones, 1.0).then_inc(setup_done, 1)
                for s in range(2):
                    nc.vector.memset(k_stack[s][STACK:ROWS, :, :], 1.0).then_inc(ones_set, 1)
                dve.wait_ge(loaded, 16 * N_LOADS)
                dve.wait_ge(setup_done, 3)
                for g in range(4):
                    nc.vector.tensor_scalar(probs[:, 0, P * g:P * (g + 1)], ones, bv_pad[:, g:g + 1], None,
                                            ALU.mult).then_inc(bv_spread, 1)
                dve.wait_ge(bo_product, 1)
                nc.vector.tensor_tensor(bo_row[:, :], o_ps[:, 0:D], bo_row[:, :], ALU.add).then_inc(bo_made, 1)
                for stage in range(STAGES):
                    x_moments(0, stage)
                for m in range(len(M_STEPS)):
                    read_rows(0, 0, m)
                negate_maxima(0, 0)
                for m in range(EARLY):
                    read_rows(0, 1, m)

            def quarter(b, q, start, steps):
                first, last = (isinstance(b, int) and b == n for n in (0, B - 1))
                bm, qm = (b, q + 1) if q < 3 else (b + 1, 0)
                for u, work in enumerate(plan(steps)):
                    slots = [slot for kind, slot in work if kind == "max" and maxima(b, q, slot)]
                    for slot in slots[:1]:
                        read_rows(*maxima(b, q, slot))
                    if u in (2, 3) and not (first and q == 0):
                        invert_denominators(*((b, q - 1) if q > 0 else (b - 1, 3)), u - 2)
                    if q == 1 and not last and X_UNIT <= u < X_UNIT + STAGES:
                        x_moments(b + 1, u - X_UNIT)
                    for k, kind, arg in at(steps, u - 1):
                        if kind == "w1":
                            finish_silu(b - 1, start, k, arg)
                    for k, (_, end, kind, arg) in enumerate(steps):
                        if kind == "wo" and end < u < end + STAGES:
                            sum_moments(b - 1, start, k, arg, u - end)
                    for slot in slots[1:]:
                        read_rows(*maxima(b, q, slot))
                    if u == M_END - 1 and not (last and q == 3):
                        negate_maxima(bm, qm)
                    for k, kind, arg in at(steps, u):
                        if kind in ("wo", "w2"):
                            add_step(b - 1, start, k, kind, arg)
                        if kind == "wo":
                            sum_moments(b - 1, start, k, arg, 0)

            def epilogue(start):
                for stage in range(2):
                    invert_denominators(B - 1, 3, stage)
                for k, (_, _, kind, arg) in enumerate(EPILOGUE):
                    if kind in ("wo", "w2"):
                        add_step(B - 1, start, k, kind, arg)
                    if kind == "wo":
                        for stage in range(STAGES):
                            sum_moments(B - 1, start, k, arg, stage)
                    if kind == "w1":
                        finish_silu(B - 1, start, k, arg)

            walk(dve, prologue, quarter, epilogue, [(seq, DVE_SEQ_PER_BATCH)])

        @block.tensor
        def _(pe):
            def side_product(b, s, start, k, kind, arg, product, n, last):
                i, j = product
                if n == 0:
                    wait(pe, side_read, step_value(start, k - 1))
                    if kind == "ctx":
                        pe.wait_ge(ctx_landed[arg[0] % 2], b * 32 + 16 * (arg[0] // 2 + 1))
                    elif kind == "turn":
                        pe.wait_ge(max_negated, b)
                    elif kind == "x":
                        pe.wait_ge(xn_ready, b + 1)
                    elif kind == "wo":
                        pe.wait_ge(att_ready, b * 4 + 4)
                    elif kind == "h":
                        pe.wait_ge(h_ready, b * 2 + (arg + 1))
                    elif kind == "w2":
                        pe.wait_ge(silu_done, b * 8 + 4 * (arg + 1))
                if kind == "ctx":
                    c, rows = arg[0], keys_in(i)
                    t = i - 4 * c
                    ins = nc.tensor.transpose(side[:, P * t:P * t + rows], ctx_nat[0:rows, c % 2, t, P * j:P * (j + 1)],
                                              ident[0:rows, 0:rows])
                elif kind == "turn":
                    ins = nc.tensor.matmul(side[0:4 * PARTS, P * i:P * (i + 1)],
                                           neg_parts[:, i, :, :].rearrange("p a h -> p (a h)"), ident_bf[:, :],
                                           start=True, stop=True)
                elif kind == "x":
                    ins = nc.tensor.transpose(side[:, P * i:P * (i + 1)], x_nat[:, i, P * arg:P * (arg + 1)], ident[:, :])
                elif kind == "k":
                    ins = nc.tensor.matmul(side[:, 0:width(arg)], wk_sb[:, j, P * s:P * (s + 1)],
                                           ctxT[:, j, CHUNK * arg:CHUNK * arg + width(arg)],
                                           start=(j == 0), stop=(j == KC - 1))
                elif kind == "q":
                    ins = nc.tensor.matmul(side[:, :], wq_sb[:, j, P * s:P * (s + 1)], qnT[:, j, :],
                                           start=(j == 0), stop=(j == KC - 1))
                elif kind == "v":
                    rows, t = keys_in(i), i - 4 * arg
                    ins = nc.tensor.matmul(side[0:rows, P * t:P * (t + 1)], ctxT[:, j, P * i:P * i + rows],
                                           wv_sb[:, j, P * s:P * (s + 1)], start=(j == 0), stop=(j == KC - 1))
                elif kind == "wo":
                    q0 = QH * arg + P * i
                    ins = nc.tensor.matmul(side[:, D * i:D * (i + 1)], attT[:, j, q0:q0 + P], wo_pad[:, j, :],
                                           start=(j == 0), stop=(j == 3))
                elif kind == "h":
                    ins = nc.tensor.transpose(side[:, QH * i + P * j:QH * i + P * (j + 1)], h_nat[:, j, P * i:P * (i + 1)],
                                              ident[:, :])
                elif kind == "w1":
                    m = 2 * arg[1] + i
                    ins = nc.tensor.matmul(side[:, QH * i:QH * (i + 1)], w1_sb[:, j, P * m:P * (m + 1)], hT[:, j, :],
                                           start=(j == 0), stop=(j == KC - 1))
                else:
                    ins = nc.tensor.matmul(side[:, D * i:D * (i + 1)], ffT[:, j, P * i:P * (i + 1)], w2_sb[:, j, :],
                                           start=(j == 0), stop=(j == FM - 1))
                if last:
                    ins.then_inc(side_ready, 1)

            def side_step(b, s, start, k, kind, arg):
                todo = products(kind, arg)
                for n, product in enumerate(todo):
                    side_product(b, s, start, k, kind, arg, product, n, n == len(todo) - 1)

            def make_rows(b, q, m):
                r, c = M_STEPS[m]
                s = q // 2
                if m == 0:
                    pe.wait_ge(placed[q], (b + 1) * (16 * PLACED))
                    pe.wait_ge(stack_landed[q], (b + 1) * (16 * REPEATED))
                wait(pe, rows_read, per_quarter(len(M_STEPS), b, q, m - 1))
                for row in [r] if c is not None else range(r - 3, r + 1):
                    t, h = row // 4, 4 * (q % 2) + row % 4
                    k0, w, d0 = (CHUNK * c, CHUNK, 0) if c is not None else (CHUNK * (NCH - 1), TAIL, TAIL * (row - r + 3))
                    last = nc.tensor.matmul(rows_ps[:, m % 2, d0:d0 + w], q_stack[s][0:STACK, h, P * t:P * (t + 1)],
                                            k_stack[s][0:STACK, h, k0:k0 + w], start=True, stop=True)
                last.then_inc(rows_ready, 1)

            def make_scores(b, q, u, n):
                t, s = u // 2, q // 2
                if n == 0:
                    if u == 0:
                        pe.wait_ge(shift_landed, per_quarter(16 * PARTS, b, q, 16 * PARTS))
                    wait(pe, exp_done, per_quarter(UNITS, b, q, u - 1))
                j = 2 * (u % 2) + n
                h = 4 * (q % 2) + j
                ins = nc.tensor.matmul(scores[0:keys_in(t), LQ * j:LQ * (j + 1)],
                                       k_stack[s][:, h, P * t:P * t + keys_in(t)], q_stack[s][:, h, :],
                                       start=True, stop=True)
                if n == 1:
                    ins.then_inc(scores_ready, 1)

            def multiply_v(b, q, t):
                pe.wait_ge(exp_done, per_quarter(UNITS, b, q, 2 * t + 2))
                if t == 0:
                    wait(pe, o_copied, per_quarter(1, b, q, 0))
                    if isinstance(b, int) and b == q == 0:
                        pe.wait_ge(bo_made, 1)
                rows = keys_in(t)
                for j in range(4):
                    col = VH * (4 * (q % 2) + j)
                    last = nc.tensor.matmul(o_ps[32 * j:32 * j + 32, :], v_sb[q // 2][0:rows, t, col:col + 32],
                                            probs[0:rows, (q + t) % 2, LQ * j:LQ * (j + 1)],
                                            start=(t == 0), stop=(t == KT - 1))
                last.then_inc(pv_done, 1)

            def prologue():
                pe.wait_ge(ident_made, 3)
                n, m = 0, 0
                for q in (1, 2, 3):
                    for k, (_, _, kind, arg) in enumerate(PREPARE[q]):
                        if (q, kind, arg) == (1, "k", 0):
                            pe.wait_ge(ones_set, 4)
                            pe.wait_ge(loaded, 16 * N_LOADS)
                            pe.wait_ge(bv_spread, 4)
                            for g in range(4):
                                last = nc.tensor.matmul(o_ps[:, 0:D], probs[:, 0, P * g:P * (g + 1)], wo_pad[:, g, :],
                                                        start=(g == 0), stop=(g == 3))
                            last.then_inc(bo_product, 1)
                        if q == 3:
                            while m < FIRST_MAXIMA + 5 * k:
                                make_rows(0, 0, m)
                                m += 1
                        side_step(0, PREPARED[q][1], (0, n), k, kind, arg)
                    n += len(PREPARE[q])
                for m in range(m, len(M_STEPS)):
                    make_rows(0, 0, m)
                side_step(1, None, (0, BEFORE - 1), 0, "turn", 0)
                for m in range(EARLY):
                    make_rows(0, 1, m)

            def quarter(b, q, start, steps):
                bm, qm = (b, q + 1) if q < 3 else (b + 1, 0)
                ahead, s = PREPARED[q]
                for u, work in enumerate(plan(steps)):
                    for what, arg in work:
                        if what == "scores":
                            make_scores(b, q, u, arg)
                        elif what == "max":
                            if maxima(b, q, arg):
                                make_rows(*maxima(b, q, arg))
                        elif what == "side":
                            kind = arg[1]
                            if kind == "turn":
                                side_product(per_quarter(1, bm, qm, 1), None, start, *arg)
                            elif kind in ("wo", "h", "w1", "w2"):
                                side_product(b - 1, None, start, *arg)
                            else:
                                side_product(b + ahead, s, start, *arg)
                        elif u > 1:
                            multiply_v(b, q, u // 2 - 1)
                        elif q > 0:
                            multiply_v(b, q - 1, KT - 1)
                        elif not (isinstance(b, int) and b == 0):
                            multiply_v(b - 1, 3, KT - 1)

            def epilogue(start):
                multiply_v(B - 1, 3, KT - 1)
                for k, (_, _, kind, arg) in enumerate(EPILOGUE):
                    side_step(B - 1, None, start, k, kind, arg)

            walk(pe, prologue, quarter, epilogue)


_W = "L0_xattn_"
_INS = ["x", "ctx_1024", _W + "Wq", _W + "bq", _W + "Wk", _W + "bk", _W + "Wv", _W + "bv", _W + "Wo", _W + "bo",
        _W + "W1", _W + "b1", _W + "W2", _W + "b2", _W + "ln_q_g", _W + "ln_q_b", _W + "ln_ff_g", _W + "ln_ff_b"]


def kernel(**inputs):
    import numpy as np
    import concourse.bacc as bacc
    from concourse.bass_utils import run_bass_kernel_spmd

    nc = bacc.Bacc("TRN2", target_bir_lowering=False, num_devices=1)
    arrays, args = {}, []
    for name in _INS:
        a = np.ascontiguousarray(inputs[name])
        arrays[f"in_{name}"] = a
        args.append(nc.dram_tensor(f"in_{name}", a.shape, mybir.dt.from_np(a.dtype), kind="ExternalInput").ap())
    args.append(nc.dram_tensor("out", (B, LQ, D), F32, kind="ExternalOutput").ap())
    xattn_kernel(nc, *args)
    return run_bass_kernel_spmd(nc, [arrays], core_ids=[0]).results[0]["out"]
```
